# Optimizing a Trainium2 kernel written in Bass

```python
import numpy as np
import jax
import jax.numpy as jnp

def _softmax(x, axis=-1):
    return jax.nn.softmax(x, axis=axis)

def _gelu(x):
    return jax.nn.gelu(x, approximate=True)

def _silu(x):
    return jax.nn.silu(x)

def _sigmoid(x):
    return jax.nn.sigmoid(x)

def _layernorm(x, axis=-1, eps=1e-05):
    m = jnp.mean(x, axis=axis, keepdims=True)
    v = jnp.var(x, axis=axis, keepdims=True)
    return (x - m) / jnp.sqrt(v + eps)

def _scatter_add(tgt, idx, src, axis=0):
    return tgt.at[idx].add(src)

def _segment_sum(src, seg, n):
    return jax.ops.segment_sum(src, seg, n)
kernel_name = 'mk_cond_seq_d1_seqx_r2_1c7d14'

def setup_inputs(seed: int=0):
    np.random.seed(seed)
    _w = jnp.asarray

    def _rec_inputs():
        import jax
        import jax.numpy as jnp
        _rk = jax.random.key(seed)
        x = -0.0003929 + 0.9999 * jax.random.normal(jax.random.fold_in(_rk, 1), (4, 1024, 512), jnp.float32)
        _lenS = 1024 - jax.random.randint(jax.random.fold_in(_rk, 7), (4,), 0, max(1, 1024 // 4) + 1, jnp.int32)
        _lenS2 = 1024 - jax.random.randint(jax.random.fold_in(_rk, 8), (4,), 0, max(1, 1024 // 4) + 1, jnp.int32)
        cond_1024 = 0.00782532 + 1.00527 * jax.random.normal(jax.random.fold_in(_rk, 11), (4, 512), jnp.float32)
        return (x, cond_1024)
    x, cond_1024 = _rec_inputs()

    def _L0_cond_setup():
        import jax, jax.numpy as jnp
        import numpy as np
        B, L, D, P = (8, 1024, 512, 128)

        def _ln(x):
            m = x.mean(-1, keepdims=True)
            v = x.var(-1, keepdims=True)
            return (x - m) * jax.lax.rsqrt(v + 1e-05)

        def _s5(u, Lam_re, Lam_im, B_re, B_im, C_re, C_im, D_diag, log_step):
            Lam = Lam_re + 1j * Lam_im
            dt = jnp.exp(log_step)
            Lam_bar = jnp.exp(Lam * dt)
            Bc = B_re + 1j * B_im
            B_bar = ((Lam_bar - 1.0) / Lam)[:, None] * Bc
            Bu = jnp.einsum('bld,pd->blp', u.astype(B_bar.dtype), B_bar)
            A = jnp.broadcast_to(Lam_bar, Bu.shape)

            def binop(e1, e2):
                a1, b1 = e1
                a2, b2 = e2
                return (a1 * a2, a2 * b1 + b2)
            _, xs = jax.lax.associative_scan(binop, (A, Bu), axis=1)
            Cc = C_re + 1j * C_im
            return 2.0 * jnp.einsum('blp,dp->bld', xs, Cc).real + D_diag * u
        key = jax.random.key(seed)
        ks = jax.random.split(key, 16)
        inp = {'y': jax.random.normal(ks[0], (B, L, D), jnp.float32), 't': jax.random.normal(ks[1], (B, D), jnp.float32), 'Wm': jax.random.normal(ks[2], (D, 6 * D), jnp.float32) * 0.02, 'bm': jax.random.normal(ks[3], (6 * D,), jnp.float32) * 0.02, 'Lam_re': -0.5 * jnp.ones((P,), jnp.float32), 'Lam_im': jnp.pi * jnp.arange(P, dtype=jnp.float32), 'B_re': jax.random.normal(ks[4], (P, D), jnp.float32) / np.sqrt(D), 'B_im': jax.random.normal(ks[5], (P, D), jnp.float32) / np.sqrt(D), 'C_re': jax.random.normal(ks[6], (D, P), jnp.float32) / np.sqrt(P), 'C_im': jax.random.normal(ks[7], (D, P), jnp.float32) / np.sqrt(P), 'D_diag': jax.random.normal(ks[8], (D,), jnp.float32), 'log_step': jax.random.uniform(ks[9], (P,), jnp.float32, np.log(0.001), np.log(0.1)), 'Wc': jax.random.normal(ks[10], (D, 2 * D), jnp.float32) * 0.02, 'bc': jax.random.normal(ks[11], (2 * D,), jnp.float32) * 0.02, 'W1': jax.random.normal(ks[12], (D, 4 * D), jnp.float32) / np.sqrt(D), 'b1': jnp.zeros((4 * D,), jnp.float32), 'W2': jax.random.normal(ks[13], (4 * D, D), jnp.float32) / np.sqrt(4 * D) * 0.1, 'b2': jnp.zeros((D,), jnp.float32)}
        return inp
    _L0_cond_all = _L0_cond_setup()
    _L0_cond_in = {k: v for k, v in _L0_cond_all.items() if k in ('Wm', 'bm', 'Lam_re', 'Lam_im', 'B_re', 'B_im', 'C_re', 'C_im', 'D_diag', 'log_step', 'Wc', 'bc', 'W1', 'b1', 'W2', 'b2')}
    del _L0_cond_all
    return {'x': x, 'cond_1024': cond_1024, 'L0_cond_Wm': _L0_cond_in['Wm'], 'L0_cond_bm': _L0_cond_in['bm'], 'L0_cond_Lam_re': _L0_cond_in['Lam_re'], 'L0_cond_Lam_im': _L0_cond_in['Lam_im'], 'L0_cond_B_re': _L0_cond_in['B_re'], 'L0_cond_B_im': _L0_cond_in['B_im'], 'L0_cond_C_re': _L0_cond_in['C_re'], 'L0_cond_C_im': _L0_cond_in['C_im'], 'L0_cond_D_diag': _L0_cond_in['D_diag'], 'L0_cond_log_step': _L0_cond_in['log_step'], 'L0_cond_Wc': _L0_cond_in['Wc'], 'L0_cond_bc': _L0_cond_in['bc'], 'L0_cond_W1': _L0_cond_in['W1'], 'L0_cond_b1': _L0_cond_in['b1'], 'L0_cond_W2': _L0_cond_in['W2'], 'L0_cond_b2': _L0_cond_in['b2']}

def reference(x, cond_1024, L0_cond_Wm, L0_cond_bm, L0_cond_Lam_re, L0_cond_Lam_im, L0_cond_B_re, L0_cond_B_im, L0_cond_C_re, L0_cond_C_im, L0_cond_D_diag, L0_cond_log_step, L0_cond_Wc, L0_cond_bc, L0_cond_W1, L0_cond_b1, L0_cond_W2, L0_cond_b2):
    import jax
    import jax.numpy as jnp

    def _L0_cond_ref(y, t, Wm, bm, Lam_re, Lam_im, B_re, B_im, C_re, C_im, D_diag, log_step, Wc, bc, W1, b1, W2, b2):
        import jax, jax.numpy as jnp
        import numpy as np
        B, L, D, P = (8, 1024, 512, 128)

        def _ln(x):
            m = x.mean(-1, keepdims=True)
            v = x.var(-1, keepdims=True)
            return (x - m) * jax.lax.rsqrt(v + 1e-05)

        def _s5(u, Lam_re, Lam_im, B_re, B_im, C_re, C_im, D_diag, log_step):
            Lam = Lam_re + 1j * Lam_im
            dt = jnp.exp(log_step)
            Lam_bar = jnp.exp(Lam * dt)
            Bc = B_re + 1j * B_im
            B_bar = ((Lam_bar - 1.0) / Lam)[:, None] * Bc
            Bu = jnp.einsum('bld,pd->blp', u.astype(B_bar.dtype), B_bar)
            A = jnp.broadcast_to(Lam_bar, Bu.shape)

            def binop(e1, e2):
                a1, b1 = e1
                a2, b2 = e2
                return (a1 * a2, a2 * b1 + b2)
            _, xs = jax.lax.associative_scan(binop, (A, Bu), axis=1)
            Cc = C_re + 1j * C_im
            return 2.0 * jnp.einsum('blp,dp->bld', xs, Cc).real + D_diag * u
        mod = t @ Wm + bm
        shift_a, scale_a, gate_a, shift_ff, scale_ff, gate_ff = jnp.split(mod, 6, axis=-1)
        y_mod = _ln(y) * (1 + scale_a[:, None]) + shift_a[:, None]
        a_y = _s5(y_mod, Lam_re, Lam_im, B_re, B_im, C_re, C_im, D_diag, log_step)
        y = y + gate_a[:, None] * a_y
        cond = t @ Wc + bc
        scale_c, shift_c = jnp.split(cond, 2, axis=-1)
        y_norm = _ln(y) * (1 + scale_c[:, None]) + shift_c[:, None]
        y_mod = y_norm * (1 + scale_ff[:, None]) + shift_ff[:, None]
        h = jax.nn.gelu(y_mod @ W1 + b1)
        ff_y = h @ W2 + b2
        return y + gate_ff[:, None] * ff_y
    x = _L0_cond_ref(x, cond_1024, L0_cond_Wm, L0_cond_bm, L0_cond_Lam_re, L0_cond_Lam_im, L0_cond_B_re, L0_cond_B_im, L0_cond_C_re, L0_cond_C_im, L0_cond_D_diag, L0_cond_log_step, L0_cond_Wc, L0_cond_bc, L0_cond_W1, L0_cond_b1, L0_cond_W2, L0_cond_b2)
    return x

_drawn_inputs = setup_inputs


def setup_inputs(seed=0):
    import zlib

    import numpy as np

    out = dict(_drawn_inputs(seed))
    spreads = {'L0_cond_Lam_re': (-0.5, 0.6), 'L0_cond_b1': (0.0, 2.0), 'L0_cond_b2': (0.0, 0.1)}
    factors = {'L0_cond_Wc': 3.112, 'L0_cond_bc': 64.0}
    for name, (base, spread) in spreads.items():
        noise = np.random.default_rng([zlib.crc32(name.encode()), seed]).standard_normal(out[name].shape)
        drawn = base * np.exp(spread * noise) if base else spread * noise
        out[name] = jnp.asarray(drawn.astype(out[name].dtype))
    for name, factor in factors.items():
        out[name] = (out[name] * factor).astype(out[name].dtype)
    return out
```

```python
from contextlib import ExitStack

import numpy as np

import concourse.bass as bass
from concourse import mybir

F32 = mybir.dt.float32
F32R = mybir.dt.float32r
I32 = mybir.dt.int32
ALU = mybir.AluOpType
ACT = mybir.ActivationFunctionType

P = 128
BATCH, LEN, D = 4, 1024, 512
STATES = 128
TOK = 512
PER_SEQ = LEN // TOK
BLOCKS = BATCH * PER_SEQ
KD = D // P
HID = 4 * D
FT = HID // P
GROUP = 4
GROUPS = FT // GROUP
LAG = 2
EPS = 1e-5

MODS = 8
FIRST_MODS = 3
A1, S1, GA, GD, A2, S2, GB, G2 = (KD * i for i in range(8))
PARAMS = 8 * KD

SM_BIAS, SM_B1, SM_B2, SM_D, SM_RE, SM_IM, SM_STEP = 0, MODS * KD, MODS * KD + FT, MODS * KD + FT + KD, \
    MODS * KD + FT + 2 * KD, MODS * KD + FT + 2 * KD + 1, MODS * KD + FT + 2 * KD + 2
SMALLS = SM_STEP + 1

COARSE, FINE = TOK // 32, 32
ANGLES = COARSE + FINE
ROUND = 1.5 * 2.0 ** 23
ROUND12 = 1.5 * 2.0 ** 11


def f32_parts(value, bits):
    parts = []
    for b in bits:
        m, e = np.frexp(value)
        part = float(np.ldexp(np.round(np.ldexp(m, b)), int(e) - b))
        parts.append(part)
        value -= part
    return parts + [float(np.float32(value))]


LN2_PARTS = f32_parts(np.log(2.0), [12])
TWO_PI_PARTS = f32_parts(2 * np.pi, [10, 10])
EXP_TERMS = [1.0 / float(np.prod(np.arange(1, k + 1))) for k in range(9)]
SIN_TERMS = [(-1.0) ** k / float(np.prod(np.arange(1, 2 * k + 2))) for k in range(7)]
COS_TERMS = [(-1.0) ** k / float(np.prod(np.arange(1, 2 * k + 1))) for k in range(8)]
RSQRT_GUESS = 0x5F3759DF


def build(nc, x_in, cond_in, small_in, mod_in, b_in, c_in, w1_in, w2_in, out):
    with ExitStack() as ctx:
        def sb(name, shape, dt=F32):
            return ctx.enter_context(nc.sbuf_tensor(name, shape, dt))

        def raw(name, shape):
            with nc.sbuf_tensor(name, shape, F32) as t:
                return t

        def sem(name):
            return ctx.enter_context(nc.semaphore(name))

        w1_raw = raw("w1_raw", [P, GROUPS, KD, TOK])
        w1_lo = sb("w1_lo", [P, GROUPS, KD, TOK], F32R)
        w1_hi = sb("w1_hi", [P, GROUPS, KD, TOK], F32R)
        mod_w = raw("mod_w", [P, MODS, KD, D])
        w2_raw = raw("w2_raw", [P, FT, D])
        w2_lo = sb("w2_lo", [P, FT, D], F32R)
        w2_hi = sb("w2_hi", [P, FT, D], F32R)
        b_raw = raw("b_raw", [P, KD, 2, STATES])
        b_lo = sb("b_lo", [P, KD, 2, STATES], F32R)
        b_hi = sb("b_hi", [P, KD, 2, STATES], F32R)
        c_raw = raw("c_raw", [P, 2, D])
        c_lo = sb("c_lo", [P, 2, D], F32R)
        c_hi = sb("c_hi", [P, 2, D], F32R)

        y = sb("y", [P, 2, KD, TOK])
        t = sb("t", [P, KD, TOK])
        u2_hi = sb("u2_hi", [P, KD, TOK], F32R)
        u2_lo = sb("u2_lo", [P, KD, TOK], F32R)
        s_hi = sb("s_hi", [P, 2, TOK], F32R)
        s_lo = sb("s_lo", [P, 2, TOK], F32R)
        h_hi = sb("h_hi", [P, 2, TOK], F32R)
        h_lo = sb("h_lo", [P, 2, TOK], F32R)
        q = sb("q", [P, 2, TOK])
        r = sb("r", [P, TOK])

        small = sb("small", [P, SMALLS])
        cond = sb("cond", [P, KD, BATCH])
        params = sb("params", [P, BATCH, PARAMS])
        front_par = sb("front_par", [P, PARAMS])
        gate_now = sb("gate_now", [P, KD])
        scratch = sb("scratch", [P, 3, KD, BATCH])
        mean_w = sb("mean_w", [P, P])
        out_c, out_s = sb("out_c", [P, TOK]), sb("out_s", [P, TOK])
        in_c, in_s = sb("in_c", [P, TOK]), sb("in_s", [P, TOK])
        state = sb("state", [P, 2])
        col = sb("col", [P, 24])
        coli = sb("coli", [P, 1], I32)
        ramp_i = sb("ramp_i", [P, ANGLES], I32)
        ang = sb("ang", [P, 6, ANGLES])

        acc = [ctx.enter_context(nc.psum_tensor(f"acc{m}", [P, TOK], F32)) for m in range(KD)]
        hid = [ctx.enter_context(nc.psum_tensor(f"hid{m}", [P, TOK], F32)) for m in range(2)]
        aux = [ctx.enter_context(nc.psum_tensor(f"aux{m}", [P, TOK], F32)) for m in range(2)]
        mod_ps = acc[0]

        small_in_sem, cond_in_sem = sem("small_loaded"), sem("cond_loaded")
        mod_loaded = [sem(f"mod_loaded{c}") for c in range(MODS)]
        b_loaded, c_loaded = sem("b_loaded"), sem("c_loaded")
        w1_loaded = [sem(f"w1_loaded{g}") for g in range(GROUPS)]
        w2_loaded = [sem(f"w2_loaded{g}") for g in range(GROUPS)]
        x_loaded = [[sem(f"x_loaded{s}_{k}") for k in range(KD)] for s in range(2)]
        y_stored = [sem(f"y_stored{k}") for k in range(KD)]
        mean_w_set = sem("mean_w_set")
        mods_done = sem("mods_done")
        b_hi_done, c_hi_done, w1_hi_done, w2_hi_done = (sem(f"{n}_hi_done") for n in ("b", "c", "w1", "w2"))
        b_split, c_split, w1_split, w2_split = (sem(f"{n}_split") for n in ("b", "c", "w1", "w2"))
        table_step = sem("table_step")
        tables_pool = sem("tables_pool")
        table_dve = sem("table_dve")
        params_step = sem("params_step")
        half_sum = sem("half_sum")
        chunk_sum = sem("chunk_sum")
        mean_ready = sem("mean_ready")
        centered = sem("centered")
        squared = sem("squared")
        square_pair = sem("square_pair")
        square_sum = sem("square_sum")
        var_ready = sem("var_ready")
        newton = sem("newton")
        normed = sem("normed")
        modulated = sem("modulated")
        u1_hi_done, u1_lo_done = sem("u1_hi_done"), sem("u1_lo_done")
        skip_added = sem("skip_added")
        b_done = sem("b_done")
        rot = sem("rot")
        carried = sem("carried")
        x_hi_done, x_lo_done = sem("x_hi_done"), sem("x_lo_done")
        c_done = sem("c_done")
        y_mid = sem("y_mid")
        y_biased = sem("y_biased")
        u2_hi_done, u2_lo_done = sem("u2_hi_done"), sem("u2_lo_done")
        w1_done = sem("w1_done")
        gelu_done = sem("gelu_done")
        h_hi_done, h_lo_done = sem("h_hi_done"), sem("h_lo_done")
        w2_done = sem("w2_done")
        acc_done = sem("acc_done")
        y_out = sem("y_out")
        NEWTON_FIRST, NEWTON = 1 + 3, 1 + 3 * 3
        ROT = 14

        def each_block(eng, block):
            block(0, 0)
            with eng.Fori(0, (BLOCKS - 2) // 2) as i:
                block(i * 2 + 1, 1)
                block(i * 2 + 2, 0)
            block(BLOCKS - 1, 1)

        is_last = lambda n: isinstance(n, int) and n == BLOCKS - 1
        is_first = lambda n: isinstance(n, int) and n == 0

        block = ctx.enter_context(nc.Block())

        @block.sync
        def _(sp):
            sp.dma_start(small[:], small_in).then_inc(small_in_sem, 16)
            sp.dma_start(cond[:], cond_in).then_inc(cond_in_sem, 16)

            def load_x(n, s):
                for k in range(KD):
                    if not (isinstance(n, int) and n < 2):
                        sp.wait_ge(y_stored[k], n * 16 - 16)
                    sp.dma_start(y[:, s, k, :], x_in[n, :, k, :]).then_inc(x_loaded[s][k], 16)

            def load_mod(c):
                sp.dma_start(mod_w[:, c], mod_in[c]).then_inc(mod_loaded[c], 16)

            load_x(0, 0)
            for c in range(FIRST_MODS):
                load_mod(c)
            sp.dma_start(b_raw[:], b_in).then_inc(b_loaded, 16)
            sp.dma_start(c_raw[:], c_in).then_inc(c_loaded, 16)
            for g in range(GROUPS):
                sp.dma_start(w1_raw[:, g], w1_in[g]).then_inc(w1_loaded[g], 16)
            for c in range(FIRST_MODS, MODS):
                load_mod(c)
            load_x(1, 1)
            for g in range(GROUPS):
                sp.wait_ge(mods_done, g + 1)
                sp.dma_start(w2_raw[:, g * GROUP:(g + 1) * GROUP], w2_in[:, g * GROUP:(g + 1) * GROUP])\
                    .then_inc(w2_loaded[g], 16)

            def io(n, s):
                for k in range(KD):
                    sp.wait_ge(y_out, n * KD + k + 1)
                    sp.dma_start(out[n, :, k, :], y[:, s, k, :]).then_inc(y_stored[k], 16)

            io(0, 0)
            load_x(2, 0)
            with sp.Fori(0, (BLOCKS - 4) // 2) as i:
                for j, s in ((1, 1), (2, 0)):
                    io(i * 2 + j, s)
                    load_x(i * 2 + j + 2, s)
            io(BLOCKS - 3, 1)
            load_x(BLOCKS - 1, 1)
            io(BLOCKS - 2, 0)
            io(BLOCKS - 1, 1)
            for k in range(KD):
                sp.wait_ge(y_stored[k], 16 * BLOCKS)

        @block.gpsimd
        def _(pool):
            nc.gpsimd.memset(mean_w[:], 1.0 / D).then_inc(mean_w_set, 1)
            steps = [0]

            def then(ins):
                steps[0] += 1
                ins.then_inc(table_step, 1)
                pool.wait_ge(table_step, steps[0])

            def ts(o, a, s1, s2, op0=ALU.mult, op1=ALU.add):
                then(nc.gpsimd.tensor_scalar(o, a, s1, s2, op0, op1))

            def tt(o, a, b, op):
                then(nc.gpsimd.tensor_tensor(o, a, b, op))

            c = lambda i: col[:, i:i + 1]
            re, im, step = (small[:, i:i + 1] for i in (SM_RE, SM_IM, SM_STEP))
            then(nc.gpsimd.iota(ramp_i[:, 0:COARSE], pattern=[[FINE, COARSE]], base=0, channel_multiplier=0))
            then(nc.gpsimd.iota(ramp_i[:, COARSE:ANGLES], pattern=[[1, FINE]], base=1, channel_multiplier=0))
            j = ang[:, 0]
            then(nc.gpsimd.tensor_copy(j, ramp_i[:]))
            pool.wait_ge(small_in_sem, 16)

            def exp(o, a, k, f, p):
                ts(p, a, -87.0, 88.0, ALU.max, ALU.min)
                ts(k, p, float(np.float32(1 / np.log(2.0))), ROUND)
                ts(k, k, ROUND, None, ALU.subtract, ALU.bypass)
                for part in LN2_PARTS:
                    ts(f, k, -part, None, ALU.mult, ALU.bypass)
                    tt(p, p, f, ALU.add)
                ts(f, p, EXP_TERMS[8], EXP_TERMS[7])
                for term in EXP_TERMS[6::-1]:
                    ts(f, f, p, term)
                ts(k, k, 127.0, 2.0 ** 23, ALU.add, ALU.mult)
                then(nc.gpsimd.tensor_copy(coli[:], k))
                tt(o, f, coli[:].bitcast(F32), ALU.mult)

            dt_c, r_c, th = c(0), c(1), c(2)
            exp(dt_c, step, c(3), c(4), c(5))
            tt(c(6), re, dt_c, ALU.mult)
            exp(r_c, c(6), c(3), c(4), c(5))
            tt(th, im, dt_c, ALU.mult)
            ts(c(3), th, float(np.float32(1 / (2 * np.pi))), ROUND)
            ts(c(3), c(3), ROUND, None, ALU.subtract, ALU.bypass)
            for part in TWO_PI_PARTS:
                ts(c(4), c(3), -part, None, ALU.mult, ALU.bypass)
                tt(th, th, c(4), ALU.add)
            ts(th, th, float(np.float32(1 / (2 * np.pi))), None, ALU.mult, ALU.bypass)
            ts(c(3), th, ROUND12, None, ALU.add, ALU.bypass)
            ts(c(3), c(3), ROUND12, None, ALU.subtract, ALU.bypass)
            tt(c(4), th, c(3), ALU.subtract)
            turns, whole, half = ang[:, 1], ang[:, 2], ang[:, 1]
            ts(turns, j, c(3), None, ALU.mult, ALU.bypass)
            ts(whole, turns, ROUND, None, ALU.add, ALU.bypass)
            ts(whole, whole, ROUND, None, ALU.subtract, ALU.bypass)
            tt(turns, turns, whole, ALU.subtract)
            ts(whole, j, c(4), None, ALU.mult, ALU.bypass)
            tt(turns, turns, whole, ALU.add)
            ts(half, turns, float(np.float32(np.pi)), None, ALU.mult, ALU.bypass)
            w, sn, cs = ang[:, 2], ang[:, 3], ang[:, 4]
            tt(w, half, half, ALU.mult)
            for o, terms in ((sn, SIN_TERMS), (cs, COS_TERMS)):
                ts(o, w, terms[-1], terms[-2])
                for term in terms[-3::-1]:
                    tt(o, o, w, ALU.mult)
                    ts(o, o, term, None, ALU.add, ALU.bypass)
            tt(sn, sn, half, ALU.mult)
            tt(cs, cs, sn, ALU.mult)
            tt(sn, sn, sn, ALU.mult)
            ts(ang[:, 1], cs, 2.0, None, ALU.mult, ALU.bypass)
            ts(ang[:, 2], sn, -2.0, 1.0)
            tt(c(7), re, re, ALU.mult)
            tt(c(8), im, im, ALU.mult)
            tt(c(7), c(7), c(8), ALU.add)
            nc.gpsimd.memset(c(9), 0.0).then_inc(tables_pool, 1)

            for g in range(GROUPS):
                part = slice(g * GROUP, (g + 1) * GROUP)
                pool.wait_ge(w2_hi_done, g + 1)
                nc.gpsimd.tensor_tensor(w2_lo[:, part], w2_raw[:, part], w2_hi[:, part].bitcast(F32),
                                        ALU.subtract).then_inc(w2_split, 1)

        @block.tensor
        def _(pe):
            def product(dst, w_hi, w_lo, v_hi, v_lo, first, last):
                nc.tensor.matmul(dst, w_hi, v_hi, start=first, stop=False)
                nc.tensor.matmul(dst, w_hi, v_lo, start=False, stop=False)
                return nc.tensor.matmul(dst, w_lo, v_hi, start=False, stop=last)

            def modulation(c):
                pe.wait_ge(mod_loaded[c], 16)
                for kk in range(KD):
                    o = mod_ps[:, (c * KD + kk) * BATCH:(c * KD + kk + 1) * BATCH]
                    for k in range(KD):
                        last = nc.tensor.matmul(o, mod_w[:, c, k, kk * P:(kk + 1) * P], cond[:, k, :],
                                                start=(k == 0), stop=(k == KD - 1))
                last.then_inc(mods_done, 1)

            def mean(m, ln):
                pe.wait_ge(chunk_sum, m * 2 + ln + 1)
                nc.tensor.matmul(aux[0][:], mean_w[:], r[:], start=True, stop=True).then_inc(mean_ready, 1)

            def variance(m, ln):
                pe.wait_ge(square_sum, m * 2 + ln + 1)
                nc.tensor.matmul(aux[1][:], mean_w[:], r[:], start=True, stop=True).then_inc(var_ready, 1)

            def b_product(m, k):
                pe.wait_ge(u1_lo_done, m * KD + k + 1)
                for c in range(2):
                    last = product(aux[c][:], b_hi[:, k, c, :], b_lo[:, k, c, :], s_hi[:, k % 2, :],
                                   s_lo[:, k % 2, :], k == 0, k == KD - 1)
                last.then_inc(b_done, 1)

            def c_product(m, mm):
                if mm == 0:
                    pe.wait_ge(x_lo_done, m * 2 + 2)
                else:
                    if mm >= 2:
                        pe.wait_ge(y_mid, m * KD + mm - 1)
                for c in range(2):
                    part = slice(mm * P, (mm + 1) * P)
                    last = product(aux[mm % 2][:], c_hi[:, c, part], c_lo[:, c, part], s_hi[:, c, :],
                                   s_lo[:, c, :], c == 0, c == 1)
                last.then_inc(c_done, 1)

            def w1_product(n, f, half):
                if half == 0:
                    if not (is_first(n) and f < 2):
                        pe.wait_ge(h_lo_done, n * FT + f - 1)
                    if is_first(n) and f % GROUP == 0:
                        pe.wait_ge(w1_split, f // GROUP + 1)
                for k in range(half * KD // 2, (half + 1) * KD // 2):
                    if f == 0:
                        pe.wait_ge(u2_lo_done, n * KD + k + 1)
                    g, part = f // GROUP, slice(f % GROUP * P, (f % GROUP + 1) * P)
                    last = product(hid[f % 2][:], w1_hi[:, g, k, part], w1_lo[:, g, k, part], u2_hi[:, k, :],
                                   u2_lo[:, k, :], k == 0, k == KD - 1)
                if half == 1:
                    last.then_inc(w1_done, 1)

            def w2_product(n, f, half):
                if half == 0:
                    pe.wait_ge(h_lo_done, n * FT + f + 1)
                    if is_first(n) and f % GROUP == 0:
                        pe.wait_ge(w2_split, f // GROUP + 1)
                for m in range(half * KD // 2, (half + 1) * KD // 2):
                    if f == 0 and not is_first(n):
                        pe.wait_ge(y_out, n * KD - KD + m + 1)
                    part = slice(m * P, (m + 1) * P)
                    last = product(acc[m][:], w2_hi[:, f, part], w2_lo[:, f, part], h_hi[:, f % 2, :],
                                   h_lo[:, f % 2, :], f == 0, f == FT - 1)
                    if f == FT - 1:
                        last.then_inc(acc_done, 1)
                if half == 1 and f < FT - 1:
                    last.then_inc(w2_done, 1)

            pe.wait_ge(mean_w_set, 1)
            mean(0, 0)
            pe.wait_ge(cond_in_sem, 16)
            for c in range(FIRST_MODS):
                modulation(c)
            variance(0, 0)
            pe.wait_ge(b_split, 1)
            for k in range(KD):
                b_product(0, k)
            for c in range(FIRST_MODS, MODS):
                modulation(c)
            pe.wait_ge(c_split, 1)
            for mm in range(KD):
                c_product(0, mm)
            mean(0, 1)
            variance(0, 1)

            def front(m, f, quarter):
                at = (f, quarter)
                if at == (2, 3):
                    mean(m, 0)
                if at == (3, 3):
                    variance(m, 0)
                if at == (6, 1):
                    b_product(m, 0)
                if at == (6, 2):
                    b_product(m, 1)
                if at == (6, 3):
                    b_product(m, 2)
                if at == (7, 0):
                    b_product(m, 3)
                if at == (9, 1):
                    c_product(m, 0)
                    c_product(m, 1)
                if at == (9, 2):
                    c_product(m, 2)
                    c_product(m, 3)
                if at == (10, 1):
                    mean(m, 1)
                if at == (11, 2):
                    variance(m, 1)

            def feed_forward(n, s):
                for f in range(FT):
                    for half in range(2):
                        w1_product(n, f, half)
                        if not is_last(n):
                            front(n + 1, f, half)
                    if f >= LAG:
                        for half in range(2):
                            w2_product(n, f - LAG, half)
                            if not is_last(n):
                                front(n + 1, f, 2 + half)
                for f in range(FT - LAG, FT):
                    w2_product(n, f, 0)
                    w2_product(n, f, 1)

            each_block(pe, feed_forward)

        @block.scalar
        def _(act):
            def copy(o, a):
                return nc.scalar.activation(o, a, ACT.Copy)

            def squares(m, ln):
                for k, o in enumerate((q[:, 0, :], q[:, 1, :], r[:], aux[1][:])):
                    act.wait_ge(centered, m * 2 * KD + ln * KD + k + 1)
                    nc.scalar.activation(o, t[:, k, :], ACT.Square).then_inc(squared, 1)

            def modulate(m, ln, k, a, s):
                act.wait_ge(normed, m * 2 * KD + ln * KD + k + 1)
                nc.scalar.activation(t[:, k, :], t[:, k, :], ACT.Identity, bias=front_par[:, s + k:s + k + 1],
                                     scale=front_par[:, a + k:a + k + 1]).then_inc(modulated, 1)

            def s5_input(m, chunks):
                for k in chunks:
                    modulate(m, 0, k, A1, S1)
                    act.wait_ge(modulated, m * 2 * KD + k + 1)
                    if k >= 2:
                        act.wait_ge(b_done, m * KD + k - 1)
                    copy(s_hi[:, k % 2, :], t[:, k, :]).then_inc(u1_hi_done, 1)

            def states_hi(m, c):
                act.wait_ge(rot, m * ROT + (ROT - 1 if c == 0 else ROT))
                copy(s_hi[:, c, :], t[:, 2, :] if c == 0 else q[:, 0, :]).then_inc(x_hi_done, 1)

            def bias_y(m, s):
                for k in range(KD):
                    act.wait_ge(centered, m * 2 * KD + KD + k + 1)
                    nc.scalar.activation(y[:, s, k, :], y[:, s, k, :], ACT.Identity,
                                         bias=front_par[:, GB + k:GB + k + 1]).then_inc(y_biased, 1)

            def ff_input(m):
                for k in range(KD):
                    modulate(m, 1, k, A2, S2)

            def ff_input_hi(m):
                if not is_first(m):
                    act.wait_ge(w1_done, m * FT)
                for k in range(KD):
                    act.wait_ge(modulated, m * 2 * KD + KD + k + 1)
                    copy(u2_hi[:, k, :], t[:, k, :]).then_inc(u2_hi_done, 1)

            def gelu(n, f):
                act.wait_ge(w1_done, n * FT + f + 1)
                nc.scalar.activation(hid[f % 2][:], hid[f % 2][:], ACT.Gelu_apprx_tanh,
                                     bias=small[:, SM_B1 + f:SM_B1 + f + 1]).then_inc(gelu_done, 1)

            def hidden_hi(n, f):
                act.wait_ge(gelu_done, n * FT + f + 1)
                if f >= 2:
                    act.wait_ge(w2_done, n * (FT - 1) + f - 1)
                elif not is_first(n):
                    if f == 0:
                        act.wait_ge(w2_done, n * (FT - 1))
                    else:
                        act.wait_ge(acc_done, n * KD)
                copy(h_hi[:, f % 2, :], hid[f % 2][:]).then_inc(h_hi_done, 1)

            act.wait_ge(b_loaded, 16)
            copy(b_hi[:], b_raw[:]).then_inc(b_hi_done, 1)
            squares(0, 0)
            act.wait_ge(c_loaded, 16)
            copy(c_hi[:], c_raw[:]).then_inc(c_hi_done, 1)
            act.wait_ge(params_step, 3)
            s5_input(0, range(KD))
            for g in range(GROUPS):
                act.wait_ge(w1_loaded[g], 16)
                copy(w1_hi[:, g], w1_raw[:, g]).then_inc(w1_hi_done, 1)
            for c in range(2):
                states_hi(0, c)
            squares(0, 1)
            bias_y(0, 0)
            ff_input(0)
            ff_input_hi(0)
            act.wait_ge(mods_done, MODS)
            for g in range(GROUPS):
                part = slice(g * GROUP, (g + 1) * GROUP)
                act.wait_ge(w2_loaded[g], 16)
                copy(w2_hi[:, part], w2_raw[:, part]).then_inc(w2_hi_done, 1)

            def feed_forward(n, s):
                m = n + 1
                for f in range(FT):
                    gelu(n, f)
                    if not is_last(n):
                        if f == 5:
                            s5_input(m, (0, 1))
                        if f == 6:
                            s5_input(m, (2, 3))
                        if f == 8:
                            states_hi(m, 0)
                            states_hi(m, 1)
                        if f == 10:
                            squares(m, 1)
                        if f == 13:
                            ff_input(m)
                    hidden_hi(n, f)
                    if not is_last(n):
                        if f == 2:
                            squares(m, 0)
                        if f == 10:
                            bias_y(m, 1 - s)
                if not is_last(n):
                    ff_input_hi(m)

            each_block(act, feed_forward)

        @block.vector
        def _(dve):
            def tt(o, a, b, op):
                return nc.vector.tensor_tensor(o, a, b, op)

            def add(o, a, b):
                return tt(o, a, b, ALU.add)

            def sub(o, a, b):
                return tt(o, a, b, ALU.subtract)

            def mul(o, a, b):
                return tt(o, a, b, ALU.mult)

            def low(o, whole, hi):
                return sub(o, whole, hi.bitcast(F32))

            def feature_sum(m, s, ln):
                for h in range(2):
                    if ln == 0:
                        for k in (2 * h, 2 * h + 1):
                            dve.wait_ge(x_loaded[s][k], (m - s) * 8 + 16)
                    else:
                        dve.wait_ge(y_mid, m * KD + 2 * h + 2)
                    add(q[:, h, :], y[:, s, 2 * h, :], y[:, s, 2 * h + 1, :]).then_inc(half_sum, 1)
                dve.wait_ge(half_sum, m * 4 + ln * 2 + 2)
                add(r[:], q[:, 0, :], q[:, 1, :]).then_inc(chunk_sum, 1)

            def center(m, s, ln):
                dve.wait_ge(mean_ready, m * 2 + ln + 1)
                for k in range(KD):
                    sub(t[:, k, :], y[:, s, k, :], aux[0][:]).then_inc(centered, 1)
                dve.wait_ge(squared, m * 2 * KD + ln * KD + 2)
                add(q[:, 0, :], q[:, 0, :], q[:, 1, :]).then_inc(square_pair, 1)
                dve.wait_ge(squared, m * 2 * KD + ln * KD + KD)
                add(r[:], r[:], aux[1][:]).then_inc(square_pair, 1)
                dve.wait_ge(square_pair, m * 4 + ln * 2 + 2)
                nc.vector.scalar_tensor_tensor(r[:], r[:], EPS * KD, q[:, 0, :], ALU.add, ALU.add)\
                    .then_inc(square_sum, 1)

            def rsqrt(m, ln, part):
                v, e = aux[1][:], q[:, 1, :]
                at = [m * 2 * NEWTON + ln * NEWTON + (0 if part == 0 else NEWTON_FIRST)]

                def then(ins):
                    at[0] = at[0] + 1
                    ins.then_inc(newton, 1)
                    dve.wait_ge(newton, at[0])

                if part == 0:
                    dve.wait_ge(var_ready, m * 2 + ln + 1)
                    then(nc.vector.tensor_scalar(r[:].bitcast(I32), v.bitcast(I32), -0.5, float(RSQRT_GUESS),
                                                 ALU.mult, ALU.add))
                for _ in range(1 if part == 0 else 2):
                    then(mul(e, r[:], r[:]))
                    then(nc.vector.scalar_tensor_tensor(e, e, -0.5, v, ALU.mult, ALU.mult))
                    then(nc.vector.scalar_tensor_tensor(r[:], e, 1.5, r[:], ALU.add, ALU.mult))

            def normalize(m, ln):
                for k in range(KD):
                    mul(t[:, k, :], t[:, k, :], r[:]).then_inc(normed, 1)

            def s5_input_lo(m, s, chunks):
                for k in chunks:
                    dve.wait_ge(u1_hi_done, m * KD + k + 1)
                    low(s_lo[:, k % 2, :], t[:, k, :], s_hi[:, k % 2, :]).then_inc(u1_lo_done, 1)
                    nc.vector.scalar_tensor_tensor(y[:, s, k, :], t[:, k, :], front_par[:, GD + k:GD + k + 1],
                                                   y[:, s, k, :], ALU.mult, ALU.add).then_inc(skip_added, 1)

            def rotate_in(m):
                dve.wait_ge(b_done, m * KD + KD)
                dve.wait_ge(skip_added, m * KD + KD)
                z = [t[:, k, :] for k in range(KD)]
                mul(z[0], in_c[:], aux[0][:]).then_inc(rot, 1)
                mul(z[2], in_s[:], aux[1][:]).then_inc(rot, 1)
                mul(z[1], in_c[:], aux[1][:]).then_inc(rot, 1)
                mul(z[3], in_s[:], aux[0][:]).then_inc(rot, 1)
                dve.wait_ge(rot, m * ROT + 2)
                sub(z[0], z[0], z[2]).then_inc(rot, 1)
                dve.wait_ge(rot, m * ROT + 4)
                add(z[1], z[1], z[3]).then_inc(rot, 1)

            def recur(m, starts):
                z = [t[:, k, :] for k in range(KD)]
                if not starts:
                    dve.wait_ge(carried, m * 2)
                for c in range(2):
                    dve.wait_ge(rot, m * ROT + 5 + c)
                    nc.vector.tensor_tensor_scan(z[c], col[:, 1:2].to_broadcast([P, TOK]), z[c],
                                                 0.0 if starts else state[:, c:c + 1],
                                                 ALU.mult, ALU.add).then_inc(rot, 1)

            def rotate_out(m):
                z = [t[:, k, :] for k in range(KD)]
                dve.wait_ge(rot, m * ROT + 7)
                mul(z[2], out_c[:], z[0]).then_inc(rot, 1)
                mul(q[:, 0, :], out_s[:], z[0]).then_inc(rot, 1)
                dve.wait_ge(rot, m * ROT + 8)
                mul(z[3], out_s[:], z[1]).then_inc(rot, 1)
                mul(q[:, 1, :], out_c[:], z[1]).then_inc(rot, 1)
                dve.wait_ge(rot, m * ROT + 11)
                sub(z[2], z[2], z[3]).then_inc(rot, 1)
                dve.wait_ge(rot, m * ROT + 12)
                nc.vector.scalar_tensor_tensor(q[:, 0, :], q[:, 0, :], -1.0, q[:, 1, :], ALU.mult, ALU.subtract)\
                    .then_inc(rot, 1)
                dve.wait_ge(rot, m * ROT + 13)
                nc.vector.tensor_copy(state[:, 0:1], z[2][:, TOK - 1:TOK]).then_inc(carried, 1)
                dve.wait_ge(x_hi_done, m * 2 + 1)
                low(s_lo[:, 0, :], z[2], s_hi[:, 0, :]).then_inc(x_lo_done, 1)
                dve.wait_ge(rot, m * ROT + ROT)
                nc.vector.tensor_scalar(state[:, 1:2], q[:, 0, TOK - 1:TOK], -1.0, None, ALU.mult)\
                    .then_inc(carried, 1)
                dve.wait_ge(x_hi_done, m * 2 + 2)
                low(s_lo[:, 1, :], q[:, 0, :], s_hi[:, 1, :]).then_inc(x_lo_done, 1)

            def residual(m, s, k):
                dve.wait_ge(c_done, m * KD + k + 1)
                nc.vector.scalar_tensor_tensor(y[:, s, k, :], aux[k % 2][:], front_par[:, GA + k:GA + k + 1],
                                               y[:, s, k, :], ALU.mult, ALU.add).then_inc(y_mid, 1)

            def ff_input_lo(m):
                for k in range(KD):
                    dve.wait_ge(u2_hi_done, m * KD + k + 1)
                    low(u2_lo[:, k, :], t[:, k, :], u2_hi[:, k, :]).then_inc(u2_lo_done, 1)

            def hidden_lo(n, f):
                dve.wait_ge(h_hi_done, n * FT + f + 1)
                low(h_lo[:, f % 2, :], hid[f % 2][:], h_hi[:, f % 2, :]).then_inc(h_lo_done, 1)

            def output(n, s):
                for k in range(KD):
                    dve.wait_ge(acc_done, n * KD + k + 1)
                    dve.wait_ge(y_biased, n * KD + k + 1)
                    nc.vector.scalar_tensor_tensor(y[:, s, k, :], acc[k][:], gate_now[:, k:k + 1], y[:, s, k, :],
                                                   ALU.mult, ALU.add).then_inc(y_out, 1)

            def modulation(c, o, extra=0.0):
                ps = mod_ps[:, c * KD * BATCH:(c + 1) * KD * BATCH].rearrange("p (k b) -> p k b", b=BATCH)
                bias = small[:, SM_BIAS + c * KD:SM_BIAS + (c + 1) * KD].unsqueeze(2).to_broadcast([P, KD, BATCH])
                return nc.vector.scalar_tensor_tensor(o, ps, extra, bias, ALU.add, ALU.add)

            def wide(i):
                return small[:, i:i + KD].unsqueeze(2).to_broadcast([P, KD, BATCH])

            def par(i):
                return params[:, :, i:i + KD].rearrange("p b k -> p k b")

            feature_sum(0, 0, 0)
            center(0, 0, 0)
            dve.wait_ge(b_hi_done, 1)
            low(b_lo[:], b_raw[:], b_hi[:]).then_inc(b_split, 1)
            rsqrt(0, 0, 0)
            rsqrt(0, 0, 1)
            normalize(0, 0)
            dve.wait_ge(c_hi_done, 1)
            low(c_lo[:], c_raw[:], c_hi[:]).then_inc(c_split, 1)
            dve.wait_ge(mods_done, FIRST_MODS)
            modulation(0, par(S1))
            modulation(1, par(A1), 1.0)
            modulation(2, par(GA)).then_inc(params_step, 1)
            dve.wait_ge(params_step, 1)
            mul(par(GD), par(GA), wide(SM_D)).then_inc(params_step, 1)
            dve.wait_ge(params_step, 2)
            nc.vector.tensor_copy(front_par[:, 0:A2], params[:, 0, 0:A2]).then_inc(params_step, 1)
            dve.wait_ge(params_step, 3)
            s5_input_lo(0, 0, range(KD))

            dve.wait_ge(tables_pool, 1)
            def grid(i, coarse):
                if coarse:
                    return ang[:, i, 0:COARSE].unsqueeze(2).to_broadcast([P, COARSE, FINE])
                return ang[:, i, COARSE:ANGLES].unsqueeze(1).to_broadcast([P, COARSE, FINE])

            def as_grid(o):
                return o.rearrange("p (a b) -> p a b", b=FINE)

            steps = [0]

            def then(ins):
                steps[0] += 1
                ins.then_inc(table_dve, 1)
                dve.wait_ge(table_dve, steps[0])

            def c(i):
                return col[:, i:i + 1]

            mul(as_grid(out_c[:]), grid(2, True), grid(2, False)).then_inc(table_dve, 1)
            mul(as_grid(in_c[:]), grid(1, True), grid(1, False)).then_inc(table_dve, 1)
            mul(as_grid(out_s[:]), grid(1, True), grid(2, False)).then_inc(table_dve, 1)
            mul(as_grid(in_s[:]), grid(2, True), grid(1, False)).then_inc(table_dve, 1)
            steps[0] = 4
            dve.wait_ge(table_dve, 4)
            then(sub(out_c[:], out_c[:], in_c[:]))
            then(add(out_s[:], out_s[:], in_s[:]))
            re, im = small[:, SM_RE:SM_RE + 1], small[:, SM_IM:SM_IM + 1]
            then(nc.vector.reciprocal(c(10), c(7)))
            then(nc.vector.tensor_scalar(c(11), out_c[:, 0:1], c(1), 1.0, ALU.mult, ALU.subtract))
            then(mul(c(12), out_s[:, 0:1], c(1)))
            then(mul(c(13), c(12), im))
            then(nc.vector.scalar_tensor_tensor(c(13), c(11), re, c(13), ALU.mult, ALU.add))
            then(mul(c(14), c(11), im))
            then(nc.vector.scalar_tensor_tensor(c(14), c(12), re, c(14), ALU.mult, ALU.subtract))
            then(nc.vector.tensor_scalar(c(15), c(13), c(10), 2.0, ALU.mult, ALU.mult))
            then(nc.vector.tensor_scalar(c(16), c(14), c(10), 2.0, ALU.mult, ALU.mult))
            then(nc.vector.tensor_scalar(in_c[:], out_s[:], c(16), None, ALU.mult))
            then(nc.vector.scalar_tensor_tensor(in_c[:], out_c[:], c(15), in_c[:], ALU.mult, ALU.add))
            then(nc.vector.tensor_scalar(in_s[:], out_s[:], c(15), None, ALU.mult))
            then(nc.vector.scalar_tensor_tensor(in_s[:], out_c[:], c(16), in_s[:], ALU.mult, ALU.subtract))

            rotate_in(0)
            recur(0, True)
            rotate_out(0)
            for k in range(KD):
                residual(0, 0, k)
            feature_sum(0, 0, 1)
            for g in range(GROUPS):
                dve.wait_ge(w1_hi_done, g + 1)
                low(w1_lo[:, g], w1_raw[:, g], w1_hi[:, g]).then_inc(w1_split, 1)
            dve.wait_ge(mods_done, MODS)
            f1, s0, sh = (scratch[:, i] for i in range(3))
            modulation(4, f1, 1.0)
            modulation(6, par(A2), 1.0)
            modulation(7, s0)
            modulation(3, sh)
            modulation(5, par(G2)).then_inc(params_step, 1)
            dve.wait_ge(params_step, 4)
            mul(par(A2), par(A2), f1)
            mul(s0, s0, f1)
            mul(par(GB), par(G2), wide(SM_B2)).then_inc(params_step, 1)
            dve.wait_ge(params_step, 5)
            add(par(S2), s0, sh).then_inc(params_step, 1)
            dve.wait_ge(params_step, 6)
            nc.vector.tensor_copy(front_par[:, A2:PARAMS], params[:, 0, A2:PARAMS])
            nc.vector.tensor_copy(gate_now[:], params[:, 0, G2:G2 + KD]).then_inc(params_step, 1)
            center(0, 0, 1)
            rsqrt(0, 1, 0)
            rsqrt(0, 1, 1)
            normalize(0, 1)
            ff_input_lo(0)

            def feed_forward(n, s):
                m, ms = n + 1, 1 - s
                for f in range(FT):
                    hidden_lo(n, f)
                    if is_last(n):
                        continue
                    if f == 1:
                        if ms == 0:
                            seq = m // 2 if isinstance(m, int) else None
                            load_params(m, seq)
                        feature_sum(m, ms, 0)
                        center(m, ms, 0)
                    if f == 2:
                        rsqrt(m, 0, 0)
                    if f == 3:
                        rsqrt(m, 0, 1)
                    if f == 4:
                        normalize(m, 0)
                        s5_input_lo(m, ms, (0, 1))
                    if f == 5:
                        s5_input_lo(m, ms, (2, 3))
                    if f == 6:
                        rotate_in(m)
                        recur(m, ms == 0)
                    if f == 7:
                        rotate_out(m)
                    if f == 8:
                        for k in range(KD):
                            residual(m, ms, k)
                        feature_sum(m, ms, 1)
                    if f == 9:
                        center(m, ms, 1)
                    if f == 10:
                        rsqrt(m, 1, 0)
                    if f == 11:
                        rsqrt(m, 1, 1)
                    if f == 12:
                        normalize(m, 1)
                if not is_last(n):
                    ff_input_lo(m)
                output(n, s)

            def load_params(m, seq):
                nc.vector.tensor_copy(front_par[:], params[:, bass.ds(seq_of[0], 1), :].rearrange("p o c -> p (o c)"))\
                    .then_inc(params_step, 1)

            seq_of = [None]
            feed_forward(0, 0)
            with dve.Fori(0, (BLOCKS - 2) // 2) as i:
                seq_of[0] = i + 1
                feed_forward(i * 2 + 1, 1)
                dve.wait_ge(y_out, i * (2 * KD) + 2 * KD)
                nc.vector.tensor_copy(gate_now[:], params[:, bass.ds(i + 1, 1), G2:G2 + KD]
                                      .rearrange("p o c -> p (o c)")).then_inc(params_step, 1)
                dve.wait_ge(params_step, i * 2 + 9)
                feed_forward(i * 2 + 2, 0)
            feed_forward(BLOCKS - 1, 1)


def kernel(x, cond_1024, L0_cond_Wm, L0_cond_bm, L0_cond_Lam_re, L0_cond_Lam_im, L0_cond_B_re, L0_cond_B_im,
           L0_cond_C_re, L0_cond_C_im, L0_cond_D_diag, L0_cond_log_step, L0_cond_Wc, L0_cond_bc, L0_cond_W1,
           L0_cond_b1, L0_cond_W2, L0_cond_b2):
    import concourse.bacc as _bacc
    from concourse.bass_utils import run_bass_kernel_spmd as _run

    def rows(a, last):
        return np.asarray(a).reshape(-1, P, last).transpose(1, 0, 2)

    def cols(a):
        return np.asarray(a).reshape(-1, P).T

    x_blocks = np.asarray(x).reshape(BATCH, PER_SEQ, TOK, KD, P).transpose(0, 1, 4, 3, 2)
    wm = np.asarray(L0_cond_Wm).reshape(KD, P, 6, D).transpose(2, 1, 0, 3)
    wc = np.asarray(L0_cond_Wc).reshape(KD, P, 2, D).transpose(2, 1, 0, 3)
    arrays = {
        "h_x": x_blocks.reshape(BLOCKS, P, KD, TOK),
        "h_cond": rows(np.asarray(cond_1024).T, BATCH),
        "h_small": np.concatenate([cols(L0_cond_bm), cols(L0_cond_bc), cols(L0_cond_b1), cols(L0_cond_b2),
                                    cols(L0_cond_D_diag), cols(L0_cond_Lam_re), cols(L0_cond_Lam_im),
                                    cols(L0_cond_log_step)], axis=1),
        "h_mod": np.concatenate([wm, wc], axis=0),
        "h_b": np.stack([rows(np.asarray(L0_cond_B_re).T, P), rows(np.asarray(L0_cond_B_im).T, P)], axis=2),
        "h_c": np.stack([np.asarray(L0_cond_C_re).T, np.asarray(L0_cond_C_im).T], axis=1),
        "h_w1": np.asarray(L0_cond_W1).reshape(KD, P, GROUPS, TOK).transpose(2, 1, 0, 3),
        "h_w2": rows(L0_cond_W2, D),
    }
    arrays = {k: np.ascontiguousarray(a) for k, a in arrays.items()}
    nc = _bacc.Bacc("TRN2", target_bir_lowering=False, num_devices=1, dynamic_dma_scratch_size=1024)
    args = [nc.dram_tensor(k, a.shape, F32, kind="ExternalInput").ap() for k, a in arrays.items()]
    out = nc.dram_tensor("out_y", (BLOCKS, P, KD, TOK), F32, kind="ExternalOutput").ap()
    build(nc, *args, out)
    got = _run(nc, [arrays], core_ids=[0]).results[0]["out_y"]
    y = np.asarray(got).reshape(BATCH, PER_SEQ, P, KD, TOK).transpose(0, 1, 4, 3, 2)
    return np.ascontiguousarray(y.reshape(BATCH, LEN, D))
```

```python
from contextlib import ExitStack

import numpy as np

import concourse.bass as bass
from concourse import mybir

F32 = mybir.dt.float32
F32R = mybir.dt.float32r
I32 = mybir.dt.int32
ALU = mybir.AluOpType
ACT = mybir.ActivationFunctionType

P = 128
BATCH, LEN, D = 4, 1024, 512
STATES = 128
TOK = 512
PER_SEQ = LEN // TOK
BLOCKS = BATCH * PER_SEQ
KD = D // P
HID = 4 * D
FT = HID // P
GROUP = 4
GROUPS = FT // GROUP
LAG = 2
EPS = 1e-5

MODS = 8
MOD_ORDER = (1, 0, 2, 3, 4, 5, 6, 7)
FIRST_MODS = 3
A1, S1, GA, GD, A2, S2, GB, G2 = (KD * i for i in range(8))
PARAMS = 8 * KD

SM_BIAS, SM_B1, SM_B2, SM_D, SM_RE, SM_IM, SM_STEP = 0, MODS * KD, MODS * KD + FT, MODS * KD + FT + KD, \
    MODS * KD + FT + 2 * KD, MODS * KD + FT + 2 * KD + 1, MODS * KD + FT + 2 * KD + 2
SM_UNIT = SM_STEP + 1
SMALLS = SM_UNIT + BATCH

COARSE, FINE = TOK // 32, 32
ANGLES = COARSE + FINE
ROUND = 1.5 * 2.0 ** 23
ROUND12 = 1.5 * 2.0 ** 11


def f32_parts(value, bits):
    parts = []
    for b in bits:
        m, e = np.frexp(value)
        part = float(np.ldexp(np.round(np.ldexp(m, b)), int(e) - b))
        parts.append(part)
        value -= part
    return parts + [float(np.float32(value))]


LN2_PARTS = f32_parts(np.log(2.0), [12])
TWO_PI_PARTS = f32_parts(2 * np.pi, [10, 10])
EXP_TERMS = [1.0 / float(np.prod(np.arange(1, k + 1))) for k in range(9)]
SIN_TERMS = [(-1.0) ** k / float(np.prod(np.arange(1, 2 * k + 2))) for k in range(7)]
COS_TERMS = [(-1.0) ** k / float(np.prod(np.arange(1, 2 * k + 1))) for k in range(8)]
RSQRT_GUESS = 0x5F3759DF


def build(nc, x_in, cond_in, small_in, mod_in, b_in, c_in, w1_in, w2_in, out):
    with ExitStack() as ctx:
        def sb(name, shape, dt=F32):
            return ctx.enter_context(nc.sbuf_tensor(name, shape, dt))

        def raw(name, shape):
            with nc.sbuf_tensor(name, shape, F32) as t:
                return t

        def sem(name):
            return ctx.enter_context(nc.semaphore(name))

        w1_raw = raw("w1_raw", [P, GROUPS, KD, TOK])
        w1_lo = sb("w1_lo", [P, GROUPS, KD, TOK], F32R)
        w1_hi = sb("w1_hi", [P, GROUPS, KD, TOK], F32R)
        mod_w = raw("mod_w", [P, MODS, KD, D])
        w2_raw = raw("w2_raw", [P, FT, D])
        w2_lo = sb("w2_lo", [P, FT, D], F32R)
        w2_hi = sb("w2_hi", [P, FT, D], F32R)
        b_raw = raw("b_raw", [P, KD, 2, STATES])
        b_lo = sb("b_lo", [P, KD, 2, STATES], F32R)
        b_hi = sb("b_hi", [P, KD, 2, STATES], F32R)
        c_raw = raw("c_raw", [P, 2, D])
        c_lo = sb("c_lo", [P, 2, D], F32R)
        c_hi = sb("c_hi", [P, 2, D], F32R)

        y = sb("y", [P, 2, KD, TOK])
        t = sb("t", [P, KD, TOK])
        mod_rows = raw("mod_rows", [P, MODS, D])
        u2_hi = sb("u2_hi", [P, KD, TOK], F32R)
        u2_lo = sb("u2_lo", [P, KD, TOK], F32R)
        s_hi = sb("s_hi", [P, 2, TOK], F32R)
        s_lo = sb("s_lo", [P, 2, TOK], F32R)
        h_hi = sb("h_hi", [P, 2, TOK], F32R)
        h_lo = sb("h_lo", [P, 2, TOK], F32R)
        q = sb("q", [P, 2, TOK])
        r = sb("r", [P, TOK])

        small = sb("small", [P, SMALLS])
        cond = sb("cond", [P, KD, BATCH])
        params = sb("params", [P, BATCH, PARAMS])
        front_par = sb("front_par", [P, PARAMS])
        gate_now = sb("gate_now", [P, KD])
        scratch = sb("scratch", [P, 3, KD, BATCH])
        mean_w = sb("mean_w", [P, P])
        mean_wr = sb("mean_wr", [P, P], F32R)
        r_hi, r_lo = sb("r_hi", [P, TOK], F32R), sb("r_lo", [P, TOK], F32R)
        out_c, out_s = sb("out_c", [P, TOK]), sb("out_s", [P, TOK])
        in_c, in_s = sb("in_c", [P, TOK]), sb("in_s", [P, TOK])
        state = sb("state", [P, 2])
        col = sb("col", [P, 24])
        act_scratch = sb("act_scratch", [P, 1])
        coli = sb("coli", [P, 1], I32)
        ramp_i = sb("ramp_i", [P, ANGLES], I32)
        ang = sb("ang", [P, 6, ANGLES])

        acc = [ctx.enter_context(nc.psum_tensor(f"acc{m}", [P, TOK], F32)) for m in range(KD)]
        hid = [ctx.enter_context(nc.psum_tensor(f"hid{m}", [P, TOK], F32)) for m in range(2)]
        aux = [ctx.enter_context(nc.psum_tensor(f"aux{m}", [P, TOK], F32)) for m in range(2)]
        mod_ps = [hid[1] if c in (2, 7) else hid[0] for c in range(MODS)]

        small_in_sem, cond_in_sem = sem("small_loaded"), sem("cond_loaded")
        mod_loaded = [sem(f"mod_loaded{c}") for c in range(MODS)]
        b_loaded, c_loaded = sem("b_loaded"), sem("c_loaded")
        w1_loaded = [sem(f"w1_loaded{g}") for g in range(GROUPS)]
        w2_loaded = [sem(f"w2_loaded{g}") for g in range(GROUPS)]
        x_loaded = [[sem(f"x_loaded{s}_{k}") for k in range(KD)] for s in range(2)]
        y_stored = [sem(f"y_stored{k}") for k in range(KD)]
        mean_w_set = sem("mean_w_set")
        mod_product = sem("mod_product")
        mod_copied = sem("mod_copied")
        mods_done = sem("mods_done")
        b_hi_done, c_hi_done, w1_hi_done, w2_hi_done = (sem(f"{n}_hi_done") for n in ("b", "c", "w1", "w2"))
        b_split, c_split, w1_split, w2_split = (sem(f"{n}_split") for n in ("b", "c", "w1", "w2"))
        table_step = sem("table_step")
        dt_ready = sem("dt_ready")
        radius_ready = sem("radius_ready")
        gain_ready = sem("gain_ready")
        table_dve = sem("table_dve")
        params_step = sem("params_step")
        half_sum = sem("half_sum")
        chunk_sum = sem("chunk_sum")
        mean_ready = sem("mean_ready")
        centered = sem("centered")
        squared = sem("squared")
        square_pair = sem("square_pair")
        square_sum = sem("square_sum")
        var_ready = sem("var_ready")
        sum_split = sem("sum_split")
        newton = sem("newton")
        normed = sem("normed")
        modulated = sem("modulated")
        u1_hi_done, u1_lo_done = sem("u1_hi_done"), sem("u1_lo_done")
        skip_added = sem("skip_added")
        b_done = sem("b_done")
        rot = sem("rot")
        carried = sem("carried")
        x_hi_done, x_lo_done = sem("x_hi_done"), sem("x_lo_done")
        c_done = sem("c_done")
        y_mid = sem("y_mid")
        y_biased = sem("y_biased")
        u2_hi_done, u2_lo_done = sem("u2_hi_done"), sem("u2_lo_done")
        w1_done = sem("w1_done")
        gelu_done = sem("gelu_done")
        h_hi_done, h_lo_done = sem("h_hi_done"), sem("h_lo_done")
        w2_done = sem("w2_done")
        acc_done = sem("acc_done")
        y_out = sem("y_out")
        NEWTON_FIRST, NEWTON = 1 + 4, 1 + 4 + 3
        ROT = 14

        def each_block(eng, block):
            block(0, 0)
            with eng.Fori(0, (BLOCKS - 2) // 2) as i:
                block(i * 2 + 1, 1)
                block(i * 2 + 2, 0)
            block(BLOCKS - 1, 1)

        is_last = lambda n: isinstance(n, int) and n == BLOCKS - 1
        is_first = lambda n: isinstance(n, int) and n == 0

        def s5_buffer(m, k):
            if is_first(m) and k >= 2:
                return h_hi[:, k - 2, :], h_lo[:, k - 2, :]
            return s_hi[:, k % 2, :], s_lo[:, k % 2, :]

        def exponential(engine, then, o, a, k, f, p):
            def ts(o, a, s1, s2, op0=ALU.mult, op1=ALU.add):
                then(engine.tensor_scalar(o, a, s1, s2, op0, op1))

            ts(p, a, -87.0, 88.0, ALU.max, ALU.min)
            ts(k, p, float(np.float32(1 / np.log(2.0))), ROUND)
            ts(k, k, ROUND, None, ALU.subtract, ALU.bypass)
            for part in LN2_PARTS:
                ts(f, k, -part, None, ALU.mult, ALU.bypass)
                then(engine.tensor_tensor(p, p, f, ALU.add))
            ts(f, p, EXP_TERMS[8], EXP_TERMS[7])
            for term in EXP_TERMS[6::-1]:
                ts(f, f, p, term)
            ts(k, k, 127.0, 2.0 ** 23, ALU.add, ALU.mult)
            then(engine.tensor_copy(coli[:], k))
            then(engine.tensor_tensor(o, f, coli[:].bitcast(F32), ALU.mult))

        block = ctx.enter_context(nc.Block())

        @block.sync
        def _(sp):
            sp.dma_start(small[:], small_in).then_inc(small_in_sem, 16)
            sp.dma_start(cond[:], cond_in).then_inc(cond_in_sem, 16)

            def load_x(n, s):
                for k in range(KD):
                    if not (isinstance(n, int) and n < 2):
                        sp.wait_ge(y_stored[k], n * 16 - 16)
                    sp.dma_start(y[:, s, k, :], x_in[n, :, k, :]).then_inc(x_loaded[s][k], 16)

            def load_mod(c):
                sp.dma_start(mod_w[:, c], mod_in[c]).then_inc(mod_loaded[c], 16)

            def load_w1(g):
                sp.dma_start(w1_raw[:, g], w1_in[g]).then_inc(w1_loaded[g], 16)

            load_x(0, 0)
            for c in MOD_ORDER[:2]:
                load_mod(c)
            sp.dma_start(b_raw[:], b_in).then_inc(b_loaded, 16)
            for c in MOD_ORDER[2:4]:
                load_mod(c)
            sp.dma_start(c_raw[:], c_in).then_inc(c_loaded, 16)
            load_mod(MOD_ORDER[4])
            load_w1(0)
            for c in MOD_ORDER[5:]:
                load_mod(c)
            load_w1(1)
            load_x(1, 1)
            for g in range(2, GROUPS):
                load_w1(g)
            for g in range(GROUPS):
                sp.wait_ge(mod_product, MOD_ORDER.index(g) + 1)
                sp.dma_start(w2_raw[:, g * GROUP:(g + 1) * GROUP], w2_in[:, g * GROUP:(g + 1) * GROUP])\
                    .then_inc(w2_loaded[g], 16)

            def io(n, s):
                for k in range(KD):
                    sp.wait_ge(y_out, n * KD + k + 1)
                    sp.dma_start(out[n, :, k, :], y[:, s, k, :]).then_inc(y_stored[k], 16)

            io(0, 0)
            load_x(2, 0)
            with sp.Fori(0, (BLOCKS - 4) // 2) as i:
                for j, s in ((1, 1), (2, 0)):
                    io(i * 2 + j, s)
                    load_x(i * 2 + j + 2, s)
            io(BLOCKS - 3, 1)
            load_x(BLOCKS - 1, 1)
            io(BLOCKS - 2, 0)
            io(BLOCKS - 1, 1)
            for k in range(KD):
                sp.wait_ge(y_stored[k], 16 * BLOCKS)

        @block.gpsimd
        def _(pool):
            nc.gpsimd.memset(mean_w[:], 1.0 / D).then_inc(mean_w_set, 1)
            pool.wait_ge(mean_w_set, 1)
            nc.gpsimd.tensor_copy(mean_wr[:], mean_w[:]).then_inc(mean_w_set, 1)
            steps = [0]

            def then(ins):
                steps[0] += 1
                ins.then_inc(table_step, 1)
                pool.wait_ge(table_step, steps[0])

            def ts(o, a, s1, s2, op0=ALU.mult, op1=ALU.add):
                then(nc.gpsimd.tensor_scalar(o, a, s1, s2, op0, op1))

            def tt(o, a, b, op):
                then(nc.gpsimd.tensor_tensor(o, a, b, op))

            c = lambda i: col[:, i:i + 1]
            re, im, step = (small[:, i:i + 1] for i in (SM_RE, SM_IM, SM_STEP))
            then(nc.gpsimd.iota(ramp_i[:, 0:COARSE], pattern=[[FINE, COARSE]], base=0, channel_multiplier=0))
            then(nc.gpsimd.iota(ramp_i[:, COARSE:ANGLES], pattern=[[1, FINE]], base=1, channel_multiplier=0))
            j = ang[:, 0]
            then(nc.gpsimd.tensor_copy(j, ramp_i[:]))
            pool.wait_ge(small_in_sem, 16)

            dt_c, r_c, th = c(0), c(1), c(2)
            exponential(nc.gpsimd, then, dt_c, step, c(3), c(4), c(5))
            nc.gpsimd.memset(c(9), 0.0).then_inc(dt_ready, 1)
            tt(th, im, dt_c, ALU.mult)
            ts(c(3), th, float(np.float32(1 / (2 * np.pi))), ROUND)
            ts(c(3), c(3), ROUND, None, ALU.subtract, ALU.bypass)
            for part in TWO_PI_PARTS:
                ts(c(4), c(3), -part, None, ALU.mult, ALU.bypass)
                tt(th, th, c(4), ALU.add)
            ts(th, th, float(np.float32(1 / (2 * np.pi))), None, ALU.mult, ALU.bypass)
            ts(c(3), th, ROUND12, None, ALU.add, ALU.bypass)
            ts(c(3), c(3), ROUND12, None, ALU.subtract, ALU.bypass)
            tt(c(4), th, c(3), ALU.subtract)
            turns, whole, half = ang[:, 1], ang[:, 2], ang[:, 1]
            ts(turns, j, c(3), None, ALU.mult, ALU.bypass)
            ts(whole, turns, ROUND, None, ALU.add, ALU.bypass)
            ts(whole, whole, ROUND, None, ALU.subtract, ALU.bypass)
            tt(turns, turns, whole, ALU.subtract)
            ts(whole, j, c(4), None, ALU.mult, ALU.bypass)
            tt(turns, turns, whole, ALU.add)
            ts(half, turns, float(np.float32(np.pi)), None, ALU.mult, ALU.bypass)
            w, sn, cs = ang[:, 2], ang[:, 3], ang[:, 4]
            tt(w, half, half, ALU.mult)
            def step_of(ins):
                steps[0] += 1
                ins.then_inc(table_step, 1)
                pool.wait_ge(table_step, steps[0] - 1)

            step_of(nc.gpsimd.tensor_scalar(cs, w, COS_TERMS[-1], COS_TERMS[-2], ALU.mult, ALU.add))
            step_of(nc.gpsimd.tensor_scalar(sn, w, SIN_TERMS[-1], SIN_TERMS[-2], ALU.mult, ALU.add))
            for sin_term, cos_term in zip(SIN_TERMS[-3::-1], COS_TERMS[-3:0:-1]):
                step_of(nc.gpsimd.tensor_tensor(cs, cs, w, ALU.mult))
                step_of(nc.gpsimd.tensor_tensor(sn, sn, w, ALU.mult))
                step_of(nc.gpsimd.tensor_scalar(cs, cs, cos_term, None, ALU.add, ALU.bypass))
                step_of(nc.gpsimd.tensor_scalar(sn, sn, sin_term, None, ALU.add, ALU.bypass))
            tt(cs, cs, w, ALU.mult)
            ts(cs, cs, COS_TERMS[0], None, ALU.add, ALU.bypass)
            tt(sn, sn, half, ALU.mult)
            tt(cs, cs, sn, ALU.mult)
            tt(sn, sn, sn, ALU.mult)
            ts(ang[:, 1], cs, 2.0, None, ALU.mult, ALU.bypass)
            ts(ang[:, 2], sn, -2.0, 1.0)
            def grid(i, coarse):
                if coarse:
                    return ang[:, i, 0:COARSE].unsqueeze(2).to_broadcast([P, COARSE, FINE])
                return ang[:, i, COARSE:ANGLES].unsqueeze(1).to_broadcast([P, COARSE, FINE])

            def as_grid(o):
                return o.rearrange("p (a b) -> p a b", b=FINE)

            def side(o, a, b, op):
                steps[0] += 1
                nc.gpsimd.tensor_tensor(o, a, b, op).then_inc(table_step, 1)

            side(as_grid(out_c[:]), grid(2, True), grid(2, False), ALU.mult)
            side(as_grid(in_c[:]), grid(1, True), grid(1, False), ALU.mult)
            side(as_grid(out_s[:]), grid(1, True), grid(2, False), ALU.mult)
            tt(as_grid(in_s[:]), grid(2, True), grid(1, False), ALU.mult)
            side(out_c[:], out_c[:], in_c[:], ALU.subtract)
            tt(out_s[:], out_s[:], in_s[:], ALU.add)
            pool.wait_ge(radius_ready, 1)
            ts(c(11), out_c[:, 0:1], r_c, 1.0, ALU.mult, ALU.subtract)
            tt(c(12), out_s[:, 0:1], r_c, ALU.mult)
            side(c(13), c(11), re, ALU.mult)
            side(c(14), c(12), im, ALU.mult)
            side(c(15), c(12), re, ALU.mult)
            tt(c(16), c(11), im, ALU.mult)
            side(c(13), c(13), c(14), ALU.add)
            tt(c(15), c(15), c(16), ALU.subtract)
            ts(c(17), c(13), c(10), 2.0, ALU.mult, ALU.mult)
            ts(c(18), c(15), c(10), 2.0, ALU.mult, ALU.mult)
            nc.gpsimd.memset(c(9), 0.0).then_inc(gain_ready, 1)
            pool.wait_ge(c_hi_done, 1)
            nc.gpsimd.tensor_tensor(c_lo[:], c_raw[:], c_hi[:].bitcast(F32), ALU.subtract).then_inc(c_split, 1)
            for g in range(GROUPS):
                pool.wait_ge(w1_hi_done, g + 1)
                nc.gpsimd.tensor_tensor(w1_lo[:, g], w1_raw[:, g], w1_hi[:, g].bitcast(F32),
                                        ALU.subtract).then_inc(w1_split, 1)
            for g in range(GROUPS):
                part = slice(g * GROUP, (g + 1) * GROUP)
                pool.wait_ge(w2_hi_done, g + 1)
                nc.gpsimd.tensor_tensor(w2_lo[:, part], w2_raw[:, part], w2_hi[:, part].bitcast(F32),
                                        ALU.subtract).then_inc(w2_split, 1)

        @block.tensor
        def _(pe):
            def product(dst, w_hi, w_lo, v_hi, v_lo, first, last):
                nc.tensor.matmul(dst, w_hi, v_hi, start=first, stop=False)
                nc.tensor.matmul(dst, w_hi, v_lo, start=False, stop=False)
                return nc.tensor.matmul(dst, w_lo, v_hi, start=False, stop=last)

            def modulation(i):
                c = MOD_ORDER[i]
                if i >= KD:
                    pe.wait_ge(mod_copied, i - KD + 1)
                pe.wait_ge(mod_loaded[c], 16)
                for k in range(KD):
                    last = nc.tensor.matmul(acc[i % KD][0:BATCH, :], cond[:, k, :], mod_w[:, c, k, :],
                                            start=(k == 0), stop=(k == KD - 1))
                last.then_inc(mod_product, 1)

            def turn(i):
                c = MOD_ORDER[i]
                pe.wait_ge(mod_copied, i + 1)
                if i == FIRST_MODS:
                    pe.wait_ge(params_step, 1)
                if i == MODS - 1:
                    pe.wait_ge(params_step, 3)
                for kk in range(KD):
                    last = nc.tensor.matmul(mod_ps[c][:, (c * KD + kk) * BATCH:(c * KD + kk + 1) * BATCH],
                                            mod_rows[0:BATCH, c, kk * P:(kk + 1) * P],
                                            small[0:BATCH, SM_UNIT:SM_UNIT + BATCH], start=True, stop=True)
                last.then_inc(mods_done, 1)

            def sum_product(m, dst):
                if is_first(m):
                    return nc.tensor.matmul(dst, mean_w[:], r[:], start=True, stop=True)
                nc.tensor.matmul(dst, mean_wr[:], r_hi[:], start=True, stop=False)
                return nc.tensor.matmul(dst, mean_wr[:], r_lo[:], start=False, stop=True)

            def mean(m, ln):
                pe.wait_ge(chunk_sum, m * 2 + ln + 1)
                sum_product(m, aux[0][:]).then_inc(mean_ready, 1)

            def variance(m, ln):
                pe.wait_ge(square_sum, m * 2 + ln + 1)
                sum_product(m, aux[1][:]).then_inc(var_ready, 1)

            def b_product(m, k):
                pe.wait_ge(u1_lo_done, m * KD + k + 1)
                for c in range(2):
                    last = product(aux[c][:], b_hi[:, k, c, :], b_lo[:, k, c, :], *s5_buffer(m, k),
                                   k == 0, k == KD - 1)
                last.then_inc(b_done, 1)

            def c_product(m, mm):
                if mm == 0:
                    pe.wait_ge(x_lo_done, m * 2 + 2)
                else:
                    if mm >= 2:
                        pe.wait_ge(y_mid, m * KD + mm - 1)
                for c in range(2):
                    part = slice(mm * P, (mm + 1) * P)
                    last = product(aux[mm % 2][:], c_hi[:, c, part], c_lo[:, c, part], s_hi[:, c, :],
                                   s_lo[:, c, :], c == 0, c == 1)
                last.then_inc(c_done, 1)

            def w1_product(n, f, half):
                if half == 0:
                    if not (is_first(n) and f < 2):
                        pe.wait_ge(h_lo_done, n * FT + f - 1)
                    if is_first(n) and f % GROUP == 0:
                        pe.wait_ge(w1_split, f // GROUP + 1)
                for k in range(half * KD // 2, (half + 1) * KD // 2):
                    if f == 0:
                        pe.wait_ge(u2_lo_done, n * KD + k + 1)
                    g, part = f // GROUP, slice(f % GROUP * P, (f % GROUP + 1) * P)
                    last = product(hid[f % 2][:], w1_hi[:, g, k, part], w1_lo[:, g, k, part], u2_hi[:, k, :],
                                   u2_lo[:, k, :], k == 0, k == KD - 1)
                if half == 1:
                    last.then_inc(w1_done, 1)

            def w2_product(n, f, half):
                if half == 0:
                    pe.wait_ge(h_lo_done, n * FT + f + 1)
                    if is_first(n) and f % GROUP == 0:
                        pe.wait_ge(w2_split, f // GROUP + 1)
                for m in range(half * KD // 2, (half + 1) * KD // 2):
                    if f == 0 and not is_first(n):
                        pe.wait_ge(y_out, n * KD - KD + m + 1)
                    part = slice(m * P, (m + 1) * P)
                    last = product(acc[m][:], w2_hi[:, f, part], w2_lo[:, f, part], h_hi[:, f % 2, :],
                                   h_lo[:, f % 2, :], f == 0, f == FT - 1)
                    if f == FT - 1:
                        last.then_inc(acc_done, 1)
                if half == 1 and f < FT - 1:
                    last.then_inc(w2_done, 1)

            pe.wait_ge(mean_w_set, 2)
            mean(0, 0)
            pe.wait_ge(cond_in_sem, 16)
            modulation(0)
            variance(0, 0)
            modulation(1)
            pe.wait_ge(small_in_sem, 16)
            turn(0)
            modulation(2)
            turn(1)
            modulation(3)
            turn(2)
            pe.wait_ge(b_split, 1)
            for k in range(KD):
                b_product(0, k)
            modulation(4)
            turn(3)
            modulation(5)
            turn(4)
            modulation(6)
            turn(5)
            pe.wait_ge(c_split, 1)
            for mm in range(KD):
                c_product(0, mm)
            turn(6)
            mean(0, 1)
            modulation(7)
            variance(0, 1)
            turn(7)

            def front(m, f, quarter):
                at = (f, quarter)
                if at == (3, 0):
                    mean(m, 0)
                if at == (4, 1):
                    variance(m, 0)
                if at == (6, 1):
                    b_product(m, 0)
                if at == (6, 2):
                    b_product(m, 1)
                if at == (6, 3):
                    b_product(m, 2)
                if at == (7, 0):
                    b_product(m, 3)
                if at == (9, 1):
                    c_product(m, 0)
                    c_product(m, 1)
                if at == (9, 2):
                    c_product(m, 2)
                    c_product(m, 3)
                if at == (10, 2):
                    mean(m, 1)
                if at == (11, 3):
                    variance(m, 1)

            def feed_forward(n, s):
                for f in range(FT):
                    for half in range(2):
                        w1_product(n, f, half)
                        if not is_last(n):
                            front(n + 1, f, half)
                    if f >= LAG:
                        for half in range(2):
                            w2_product(n, f - LAG, half)
                            if not is_last(n):
                                front(n + 1, f, 2 + half)
                for f in range(FT - LAG, FT):
                    w2_product(n, f, 0)
                    w2_product(n, f, 1)

            each_block(pe, feed_forward)

        @block.scalar
        def _(act):
            def copy(o, a):
                return nc.scalar.activation(o, a, ACT.Copy)

            def squares(m, ln):
                for k, o in enumerate((q[:, 0, :], q[:, 1, :], r[:], aux[1][:])):
                    act.wait_ge(centered, m * 2 * KD + ln * KD + k + 1)
                    nc.scalar.activation(o, t[:, k, :], ACT.Square).then_inc(squared, 1)

            def modulate(m, ln, k, a, s):
                act.wait_ge(normed, m * 2 * KD + ln * KD + k + 1)
                nc.scalar.activation(t[:, k, :], t[:, k, :], ACT.Identity, bias=front_par[:, s + k:s + k + 1],
                                     scale=front_par[:, a + k:a + k + 1]).then_inc(modulated, 1)

            def s5_input(m, chunks):
                for k in chunks:
                    modulate(m, 0, k, A1, S1)
                    act.wait_ge(modulated, m * 2 * KD + k + 1)
                    if k >= 2 and not is_first(m):
                        act.wait_ge(b_done, m * KD + k - 1)
                    copy(s5_buffer(m, k)[0], t[:, k, :]).then_inc(u1_hi_done, 1)

            def states_hi(m, c):
                act.wait_ge(rot, m * ROT + (ROT - 1 if c == 0 else ROT))
                copy(s_hi[:, c, :], t[:, 2, :] if c == 0 else q[:, 0, :]).then_inc(x_hi_done, 1)

            def bias_y(m, s):
                for k in range(KD):
                    act.wait_ge(centered, m * 2 * KD + KD + k + 1)
                    nc.scalar.activation(y[:, s, k, :], y[:, s, k, :], ACT.Identity,
                                         bias=front_par[:, GB + k:GB + k + 1]).then_inc(y_biased, 1)

            def ff_input(m):
                for k in range(KD):
                    modulate(m, 1, k, A2, S2)

            def ff_input_hi(m):
                act.wait_ge(w1_done, m * FT)
                for k in range(KD):
                    act.wait_ge(modulated, m * 2 * KD + KD + k + 1)
                    copy(u2_hi[:, k, :], t[:, k, :]).then_inc(u2_hi_done, 1)

            def gelu(n, f):
                act.wait_ge(w1_done, n * FT + f + 1)
                nc.scalar.activation(hid[f % 2][:], hid[f % 2][:], ACT.Gelu_apprx_tanh,
                                     bias=small[:, SM_B1 + f:SM_B1 + f + 1]).then_inc(gelu_done, 1)

            def hidden_hi(n, f):
                act.wait_ge(gelu_done, n * FT + f + 1)
                if f >= 2:
                    act.wait_ge(w2_done, n * (FT - 1) + f - 1)
                elif not is_first(n):
                    if f == 0:
                        act.wait_ge(w2_done, n * (FT - 1))
                    else:
                        act.wait_ge(acc_done, n * KD)
                copy(h_hi[:, f % 2, :], hid[f % 2][:]).then_inc(h_hi_done, 1)

            def mod_row(i):
                act.wait_ge(mod_product, i + 1)
                copy(mod_rows[0:BATCH, MOD_ORDER[i], :], acc[i % KD][0:BATCH, :]).then_inc(mod_copied, 1)

            def w1_part(g):
                act.wait_ge(w1_loaded[g], 16)
                copy(w1_hi[:, g], w1_raw[:, g]).then_inc(w1_hi_done, 1)

            def w2_part(g):
                if g == 0:
                    act.wait_ge(mod_product, MODS)
                part = slice(g * GROUP, (g + 1) * GROUP)
                act.wait_ge(w2_loaded[g], 16)
                copy(w2_hi[:, part], w2_raw[:, part]).then_inc(w2_hi_done, 1)

            act.wait_ge(small_in_sem, 16)
            nc.scalar.activation(act_scratch[:], small[:, SM_UNIT:SM_UNIT + 1], ACT.Gelu_apprx_tanh)
            squares(0, 0)
            act.wait_ge(b_loaded, 16)
            copy(b_hi[:], b_raw[:]).then_inc(b_hi_done, 1)
            mod_row(0)
            mod_row(1)
            mod_row(2)
            act.wait_ge(params_step, 2)
            s5_input(0, range(KD))
            mod_row(3)
            act.wait_ge(c_loaded, 16)
            copy(c_hi[:], c_raw[:]).then_inc(c_hi_done, 1)
            w1_part(0)
            mod_row(4)
            mod_row(5)
            for c in range(2):
                states_hi(0, c)
            mod_row(6)
            w1_part(1)
            w1_part(2)
            squares(0, 1)
            mod_row(7)
            w2_part(0)
            w1_part(3)
            w2_part(1)
            act.wait_ge(params_step, 11)
            for k in range(KD):
                modulate(0, 1, k, A2, S2)
                act.wait_ge(modulated, KD + k + 1)
                copy(u2_hi[:, k, :], t[:, k, :]).then_inc(u2_hi_done, 1)

            def feed_forward(n, s):
                m = n + 1
                for f in range(FT):
                    gelu(n, f)
                    if not is_last(n):
                        if f == 5:
                            s5_input(m, (0, 1))
                        if f == 6:
                            s5_input(m, (2, 3))
                        if f == 8:
                            states_hi(m, 0)
                            states_hi(m, 1)
                        if f == 10:
                            squares(m, 1)
                        if f == 13:
                            ff_input(m)
                    hidden_hi(n, f)
                    if is_first(n):
                        if f == 1:
                            bias_y(0, 0)
                        if f in (3, 7):
                            w2_part(2 if f == 3 else 3)
                    if not is_last(n):
                        if f == 2:
                            squares(m, 0)
                        if f == 10:
                            bias_y(m, 1 - s)
                if not is_last(n):
                    ff_input_hi(m)

            each_block(act, feed_forward)

        @block.vector
        def _(dve):
            def tt(o, a, b, op):
                return nc.vector.tensor_tensor(o, a, b, op)

            def add(o, a, b):
                return tt(o, a, b, ALU.add)

            def sub(o, a, b):
                return tt(o, a, b, ALU.subtract)

            def mul(o, a, b):
                return tt(o, a, b, ALU.mult)

            def low(o, whole, hi):
                return sub(o, whole, hi.bitcast(F32))

            def split_sum(m, ln, of_squares, ins, signal):
                if is_first(m):
                    ins.then_inc(signal, 1)
                    return
                at = m * 8 + (ln * 4 + of_squares * 2 - 8)
                ins.then_inc(sum_split, 1)
                dve.wait_ge(sum_split, at + 1)
                nc.vector.tensor_copy(r_hi[:], r[:]).then_inc(sum_split, 1)
                dve.wait_ge(sum_split, at + 2)
                low(r_lo[:], r[:], r_hi[:]).then_inc(signal, 1)

            def feature_sum(m, s, ln):
                for h in range(2):
                    for k in (2 * h, 2 * h + 1):
                        if ln == 0:
                            dve.wait_ge(x_loaded[s][k], (m - s) * 8 + 16)
                        else:
                            residual(m, s, k)
                    if ln == 1:
                        dve.wait_ge(y_mid, m * KD + 2 * h + 2)
                    add(q[:, h, :], y[:, s, 2 * h, :], y[:, s, 2 * h + 1, :]).then_inc(half_sum, 1)
                dve.wait_ge(half_sum, m * 4 + ln * 2 + 2)
                split_sum(m, ln, 0, add(r[:], q[:, 0, :], q[:, 1, :]), chunk_sum)

            def center(m, s, ln):
                dve.wait_ge(mean_ready, m * 2 + ln + 1)
                for k in range(KD):
                    sub(t[:, k, :], y[:, s, k, :], aux[0][:]).then_inc(centered, 1)
                dve.wait_ge(squared, m * 2 * KD + ln * KD + 2)
                add(q[:, 0, :], q[:, 0, :], q[:, 1, :]).then_inc(square_pair, 1)
                dve.wait_ge(squared, m * 2 * KD + ln * KD + KD)
                add(r[:], r[:], aux[1][:]).then_inc(square_pair, 1)
                dve.wait_ge(square_pair, m * 4 + ln * 2 + 2)
                split_sum(m, ln, 1, nc.vector.scalar_tensor_tensor(r[:], r[:], EPS * KD, q[:, 0, :],
                                                                   ALU.add, ALU.add), square_sum)

            def rsqrt(m, ln, part):
                v, e = aux[1][:], q[:, 1, :]
                at = [m * 2 * NEWTON + ln * NEWTON + (0 if part == 0 else NEWTON_FIRST)]

                def then(ins):
                    at[0] = at[0] + 1
                    ins.then_inc(newton, 1)
                    dve.wait_ge(newton, at[0])

                if part == 0:
                    dve.wait_ge(var_ready, m * 2 + ln + 1)
                    then(nc.vector.tensor_scalar(r[:].bitcast(I32), v.bitcast(I32), -0.5, float(RSQRT_GUESS),
                                                 ALU.mult, ALU.add))
                    then(mul(e, r[:], r[:]))
                    then(mul(e, e, v))
                    then(nc.vector.scalar_tensor_tensor(e, e, -10 / 3, e, ALU.add, ALU.mult))
                    then(nc.vector.scalar_tensor_tensor(r[:], e, 5.0, r[:], ALU.add, ALU.mult))
                else:
                    then(mul(e, r[:], r[:]))
                    then(nc.vector.scalar_tensor_tensor(e, e, -0.5 * 0.375 ** 3, v, ALU.mult, ALU.mult))
                    then(nc.vector.scalar_tensor_tensor(r[:], e, 1.5 * 0.375, r[:], ALU.add, ALU.mult))

            def normalize(m, ln):
                for k in range(KD):
                    mul(t[:, k, :], t[:, k, :], r[:]).then_inc(normed, 1)

            def s5_low(m, k):
                dve.wait_ge(u1_hi_done, m * KD + k + 1)
                hi, lo = s5_buffer(m, k)
                low(lo, t[:, k, :], hi).then_inc(u1_lo_done, 1)

            def skip(m, s, k):
                nc.vector.scalar_tensor_tensor(y[:, s, k, :], t[:, k, :], front_par[:, GD + k:GD + k + 1],
                                               y[:, s, k, :], ALU.mult, ALU.add).then_inc(skip_added, 1)

            def s5_input_lo(m, s, chunks):
                for k in chunks:
                    s5_low(m, k)
                    skip(m, s, k)

            def rotate_in(m):
                dve.wait_ge(b_done, m * KD + KD)
                dve.wait_ge(skip_added, m * KD + KD)
                z = [t[:, k, :] for k in range(KD)]
                mul(z[0], in_c[:], aux[0][:]).then_inc(rot, 1)
                mul(z[2], in_s[:], aux[1][:]).then_inc(rot, 1)
                mul(z[1], in_c[:], aux[1][:]).then_inc(rot, 1)
                mul(z[3], in_s[:], aux[0][:]).then_inc(rot, 1)
                dve.wait_ge(rot, m * ROT + 2)
                sub(z[0], z[0], z[2]).then_inc(rot, 1)
                dve.wait_ge(rot, m * ROT + 4)
                add(z[1], z[1], z[3]).then_inc(rot, 1)

            def recur(m, starts):
                z = [t[:, k, :] for k in range(KD)]
                if not starts:
                    dve.wait_ge(carried, m * 2)
                for c in range(2):
                    dve.wait_ge(rot, m * ROT + 5 + c)
                    nc.vector.tensor_tensor_scan(z[c], col[:, 1:2].to_broadcast([P, TOK]), z[c],
                                                 0.0 if starts else state[:, c:c + 1],
                                                 ALU.mult, ALU.add).then_inc(rot, 1)

            def rotate_out(m):
                z = [t[:, k, :] for k in range(KD)]
                dve.wait_ge(rot, m * ROT + 7)
                mul(z[2], out_c[:], z[0]).then_inc(rot, 1)
                mul(q[:, 0, :], out_s[:], z[0]).then_inc(rot, 1)
                dve.wait_ge(rot, m * ROT + 8)
                mul(z[3], out_s[:], z[1]).then_inc(rot, 1)
                mul(q[:, 1, :], out_c[:], z[1]).then_inc(rot, 1)
                dve.wait_ge(rot, m * ROT + 11)
                sub(z[2], z[2], z[3]).then_inc(rot, 1)
                dve.wait_ge(rot, m * ROT + 12)
                nc.vector.scalar_tensor_tensor(q[:, 0, :], q[:, 0, :], -1.0, q[:, 1, :], ALU.mult, ALU.subtract)\
                    .then_inc(rot, 1)
                dve.wait_ge(rot, m * ROT + 13)
                nc.vector.tensor_copy(state[:, 0:1], z[2][:, TOK - 1:TOK]).then_inc(carried, 1)
                dve.wait_ge(x_hi_done, m * 2 + 1)
                low(s_lo[:, 0, :], z[2], s_hi[:, 0, :]).then_inc(x_lo_done, 1)
                dve.wait_ge(rot, m * ROT + ROT)
                nc.vector.tensor_scalar(state[:, 1:2], q[:, 0, TOK - 1:TOK], -1.0, None, ALU.mult)\
                    .then_inc(carried, 1)
                dve.wait_ge(x_hi_done, m * 2 + 2)
                low(s_lo[:, 1, :], q[:, 0, :], s_hi[:, 1, :]).then_inc(x_lo_done, 1)

            def residual(m, s, k):
                dve.wait_ge(c_done, m * KD + k + 1)
                nc.vector.scalar_tensor_tensor(y[:, s, k, :], aux[k % 2][:], front_par[:, GA + k:GA + k + 1],
                                               y[:, s, k, :], ALU.mult, ALU.add).then_inc(y_mid, 1)

            def ff_input_lo(m):
                for k in range(KD):
                    dve.wait_ge(u2_hi_done, m * KD + k + 1)
                    low(u2_lo[:, k, :], t[:, k, :], u2_hi[:, k, :]).then_inc(u2_lo_done, 1)

            def hidden_lo(n, f):
                dve.wait_ge(h_hi_done, n * FT + f + 1)
                low(h_lo[:, f % 2, :], hid[f % 2][:], h_hi[:, f % 2, :]).then_inc(h_lo_done, 1)

            def output(n, s):
                for k in range(KD):
                    dve.wait_ge(acc_done, n * KD + k + 1)
                    dve.wait_ge(y_biased, n * KD + k + 1)
                    nc.vector.scalar_tensor_tensor(y[:, s, k, :], acc[k][:], gate_now[:, k:k + 1], y[:, s, k, :],
                                                   ALU.mult, ALU.add).then_inc(y_out, 1)

            def modulation(c, o, extra=0.0):
                ps = mod_ps[c][:, c * KD * BATCH:(c + 1) * KD * BATCH].rearrange("p (k b) -> p k b", b=BATCH)
                bias = small[:, SM_BIAS + c * KD:SM_BIAS + (c + 1) * KD].unsqueeze(2).to_broadcast([P, KD, BATCH])
                return nc.vector.scalar_tensor_tensor(o, ps, extra, bias, ALU.add, ALU.add)

            def wide(i):
                return small[:, i:i + KD].unsqueeze(2).to_broadcast([P, KD, BATCH])

            def par(i):
                return params[:, :, i:i + KD].rearrange("p b k -> p k b")

            steps = [0]

            def then(ins):
                steps[0] += 1
                ins.then_inc(table_dve, 1)
                dve.wait_ge(table_dve, steps[0])

            def c(i):
                return col[:, i:i + 1]

            def scaled(o, a, gain):
                steps[0] += 1
                nc.vector.tensor_scalar(o[:], a[:], gain, None, ALU.mult).then_inc(table_dve, 1)

            def combined(o, a, gain, op):
                steps[0] += 1
                nc.vector.scalar_tensor_tensor(o[:], a[:], gain, o[:], ALU.mult, op).then_inc(table_dve, 1)

            re, im = small[:, SM_RE:SM_RE + 1], small[:, SM_IM:SM_IM + 1]
            dve.wait_ge(small_in_sem, 16)
            then(mul(c(7), re, re))
            then(mul(c(8), im, im))
            then(add(c(7), c(7), c(8)))
            then(nc.vector.reciprocal(c(10), c(7)))
            feature_sum(0, 0, 0)
            center(0, 0, 0)
            dve.wait_ge(dt_ready, 1)
            then(mul(c(6), re, c(0)))
            exponential(nc.vector, then, c(1), c(6), c(19), c(20), c(21))
            nc.vector.memset(c(22), 0.0).then_inc(radius_ready, 1)
            rsqrt(0, 0, 0)
            rsqrt(0, 0, 1)
            dve.wait_ge(b_hi_done, 1)
            low(b_lo[:], b_raw[:], b_hi[:]).then_inc(b_split, 1)
            dve.wait_ge(mods_done, 2)
            modulation(0, par(S1))
            modulation(1, par(A1), 1.0).then_inc(params_step, 1)
            dve.wait_ge(params_step, 1)
            nc.vector.tensor_copy(front_par[:, 0:GA], params[:, 0, 0:GA]).then_inc(params_step, 1)
            normalize(0, 0)
            s5_low(0, 0)
            s5_low(0, 1)
            dve.wait_ge(mods_done, FIRST_MODS)
            modulation(2, par(GA)).then_inc(params_step, 1)
            dve.wait_ge(params_step, 3)
            mul(par(GD), par(GA), wide(SM_D)).then_inc(params_step, 1)
            dve.wait_ge(params_step, 4)
            nc.vector.tensor_copy(front_par[:, GA:A2], params[:, 0, GA:A2]).then_inc(params_step, 1)
            dve.wait_ge(params_step, 5)
            skip(0, 0, 0)
            s5_low(0, 2)
            skip(0, 0, 1)
            s5_low(0, 3)
            skip(0, 0, 2)
            skip(0, 0, 3)
            dve.wait_ge(gain_ready, 1)
            scaled(in_c, out_s, c(18))
            scaled(in_s, out_s, c(17))
            dve.wait_ge(table_dve, steps[0])
            combined(in_c, out_c, c(17), ALU.add)
            combined(in_s, out_c, c(18), ALU.subtract)
            dve.wait_ge(table_dve, steps[0])
            rotate_in(0)
            recur(0, True)
            rotate_out(0)
            feature_sum(0, 0, 1)
            center(0, 0, 1)
            f1, s0, sh = (scratch[:, i] for i in range(3))
            dve.wait_ge(mods_done, MODS - 1)
            modulation(4, f1, 1.0)
            modulation(6, par(A2), 1.0)
            modulation(3, sh)
            modulation(5, par(G2)).then_inc(params_step, 1)
            dve.wait_ge(params_step, 6)
            mul(par(A2), par(A2), f1)
            mul(par(GB), par(G2), wide(SM_B2)).then_inc(params_step, 1)
            rsqrt(0, 1, 0)
            rsqrt(0, 1, 1)
            dve.wait_ge(mods_done, MODS)
            modulation(7, s0).then_inc(params_step, 1)
            dve.wait_ge(params_step, 8)
            mul(s0, s0, f1).then_inc(params_step, 1)
            dve.wait_ge(params_step, 9)
            add(par(S2), s0, sh).then_inc(params_step, 1)
            dve.wait_ge(params_step, 10)
            nc.vector.tensor_copy(front_par[:, A2:PARAMS], params[:, 0, A2:PARAMS])
            nc.vector.tensor_copy(gate_now[:], params[:, 0, G2:G2 + KD]).then_inc(params_step, 1)
            normalize(0, 1)
            ff_input_lo(0)

            def feed_forward(n, s):
                m, ms = n + 1, 1 - s
                for f in range(FT):
                    hidden_lo(n, f)
                    if is_last(n):
                        continue
                    if f == 1:
                        if ms == 0:
                            load_params()
                        feature_sum(m, ms, 0)
                    if f == 2:
                        center(m, ms, 0)
                    if f == 3:
                        rsqrt(m, 0, 0)
                    if f == 4:
                        rsqrt(m, 0, 1)
                        normalize(m, 0)
                        s5_input_lo(m, ms, (0, 1))
                    if f == 5:
                        s5_input_lo(m, ms, (2, 3))
                    if f == 6:
                        rotate_in(m)
                        recur(m, ms == 0)
                    if f == 7:
                        rotate_out(m)
                    if f == 8:
                        feature_sum(m, ms, 1)
                    if f == 9:
                        center(m, ms, 1)
                    if f == 10:
                        rsqrt(m, 1, 0)
                    if f == 11:
                        rsqrt(m, 1, 1)
                    if f == 12:
                        normalize(m, 1)
                if not is_last(n):
                    ff_input_lo(m)
                output(n, s)

            def load_params():
                nc.vector.tensor_copy(front_par[:], params[:, bass.ds(next_seq[0], 1), :].rearrange("p o c -> p (o c)"))\
                    .then_inc(params_step, 1)

            next_seq = [None]
            feed_forward(0, 0)
            with dve.Fori(0, (BLOCKS - 2) // 2) as i:
                next_seq[0] = i + 1
                feed_forward(i * 2 + 1, 1)
                dve.wait_ge(y_out, i * (2 * KD) + 2 * KD)
                nc.vector.tensor_copy(gate_now[:], params[:, bass.ds(i + 1, 1), G2:G2 + KD]
                                      .rearrange("p o c -> p (o c)")).then_inc(params_step, 1)
                dve.wait_ge(params_step, i * 2 + 13)
                feed_forward(i * 2 + 2, 0)
            feed_forward(BLOCKS - 1, 1)


def kernel(x, cond_1024, L0_cond_Wm, L0_cond_bm, L0_cond_Lam_re, L0_cond_Lam_im, L0_cond_B_re, L0_cond_B_im,
           L0_cond_C_re, L0_cond_C_im, L0_cond_D_diag, L0_cond_log_step, L0_cond_Wc, L0_cond_bc, L0_cond_W1,
           L0_cond_b1, L0_cond_W2, L0_cond_b2):
    import concourse.bacc as _bacc
    from concourse.bass_utils import run_bass_kernel_spmd as _run

    def rows(a, last):
        return np.asarray(a).reshape(-1, P, last).transpose(1, 0, 2)

    def cols(a):
        return np.asarray(a).reshape(-1, P).T

    x_blocks = np.asarray(x).reshape(BATCH, PER_SEQ, TOK, KD, P).transpose(0, 1, 4, 3, 2)
    wm = np.asarray(L0_cond_Wm).reshape(KD, P, 6, D).transpose(2, 1, 0, 3)
    wc = np.asarray(L0_cond_Wc).reshape(KD, P, 2, D).transpose(2, 1, 0, 3)
    arrays = {
        "h_x": x_blocks.reshape(BLOCKS, P, KD, TOK),
        "h_cond": rows(np.asarray(cond_1024).T, BATCH),
        "h_small": np.concatenate([cols(L0_cond_bm), cols(L0_cond_bc), cols(L0_cond_b1), cols(L0_cond_b2),
                                    cols(L0_cond_D_diag), cols(L0_cond_Lam_re), cols(L0_cond_Lam_im),
                                    cols(L0_cond_log_step), np.eye(P, BATCH, dtype=np.float32)], axis=1),
        "h_mod": np.concatenate([wm, wc], axis=0),
        "h_b": np.stack([rows(np.asarray(L0_cond_B_re).T, P), rows(np.asarray(L0_cond_B_im).T, P)], axis=2),
        "h_c": np.stack([np.asarray(L0_cond_C_re).T, np.asarray(L0_cond_C_im).T], axis=1),
        "h_w1": np.asarray(L0_cond_W1).reshape(KD, P, GROUPS, TOK).transpose(2, 1, 0, 3),
        "h_w2": rows(L0_cond_W2, D),
    }
    arrays = {k: np.ascontiguousarray(a) for k, a in arrays.items()}
    nc = _bacc.Bacc("TRN2", target_bir_lowering=False, num_devices=1, dynamic_dma_scratch_size=1024)
    args = [nc.dram_tensor(k, a.shape, F32, kind="ExternalInput").ap() for k, a in arrays.items()]
    out = nc.dram_tensor("out_y", (BLOCKS, P, KD, TOK), F32, kind="ExternalOutput").ap()
    build(nc, *args, out)
    got = _run(nc, [arrays], core_ids=[0]).results[0]["out_y"]
    y = np.asarray(got).reshape(BATCH, PER_SEQ, P, KD, TOK).transpose(0, 1, 4, 3, 2)
    return np.ascontiguousarray(y.reshape(BATCH, LEN, D))
```
